# Optimizing a Trainium2 kernel written in Bass

```python
import numpy as np
import jax
import jax.numpy as jnp

def _softmax(x, axis=-1):
    return jax.nn.softmax(x, axis=axis)

def _gelu(x):
    return jax.nn.gelu(x, approximate=True)

def _silu(x):
    return jax.nn.silu(x)

def _sigmoid(x):
    return jax.nn.sigmoid(x)

def _layernorm(x, axis=-1, eps=1e-05):
    m = jnp.mean(x, axis=axis, keepdims=True)
    v = jnp.var(x, axis=axis, keepdims=True)
    return (x - m) / jnp.sqrt(v + eps)

def _scatter_add(tgt, idx, src, axis=0):
    return tgt.at[idx].add(src)

def _segment_sum(src, seg, n):
    return jax.ops.segment_sum(src, seg, n)
kernel_name = 'mk_xattn_ffn_d1_seqx_r8_850fe9'

def setup_inputs(seed: int=0):
    np.random.seed(seed)
    _w = jnp.asarray

    def _rec_inputs():
        import jax
        import jax.numpy as jnp
        _rk = jax.random.key(seed)
        x = 7.22e-05 + 1 * jax.random.normal(jax.random.fold_in(_rk, 1), (32, 64, 128), jnp.float32)
        _lenS = 64 - jax.random.randint(jax.random.fold_in(_rk, 7), (32,), 0, max(1, 64 // 4) + 1, jnp.int32)
        _lenS2 = 64 - jax.random.randint(jax.random.fold_in(_rk, 8), (32,), 0, max(1, 64 // 4) + 1, jnp.int32)
        _ctx_1024P = jax.random.normal(jax.random.fold_in(_rk, 11), (32, 16, 128), jnp.float32)
        _ctx_1024c = jax.random.dirichlet(jax.random.fold_in(_rk, 511), 0.3 * jnp.ones((16,), jnp.float32), (32, 64))
        _ctx_1024t = jnp.einsum('bsk,bkd->bsd', _ctx_1024c, _ctx_1024P)
        _ctx_1024t = _ctx_1024t * jax.lax.rsqrt(jnp.mean(jnp.square(_ctx_1024t)) + 1e-12) * 0.953939
        ctx_1024 = 4.13588e-05 + 0.999923 * (_ctx_1024t + 0.3 * jax.random.normal(jax.random.fold_in(_rk, 611), (32, 64, 128), jnp.float32))
        _validS = jnp.arange(64)[None, :] < _lenS[:, None]
        _validS2 = jnp.arange(64)[None, :] < _lenS2[:, None]
        _causal = jnp.tril(jnp.ones((64, 64), dtype=bool))
        mask_BxS2_ff1 = jnp.where(jnp.ones((32, 64), dtype=bool), 1.0, 0.0).astype(jnp.float32)
        return (x, ctx_1024, mask_BxS2_ff1)
    x, ctx_1024, mask_BxS2_ff1 = _rec_inputs()

    def _L0_xattn_setup():
        import jax, jax.numpy as jnp
        import numpy as np
        B, S, D = (4, 256, 128)
        H, DK, DV, DFF = (8, 128, 128, 256)
        MASK_VALUE = -1e+30
        EPS = 1e-14

        def _layernorm(x, g, b):
            mean = jnp.mean(x, axis=-1, keepdims=True)
            var = jnp.mean(jnp.square(x - mean), axis=-1, keepdims=True)
            return (x - mean) / jnp.sqrt(var + EPS) * g + b
        key = jax.random.key(seed)
        ks = jax.random.split(key, 10)

        def g(k, shape, scale=0.02):
            return jax.random.normal(k, shape, dtype=jnp.float32) * scale
        return {'query': jax.random.normal(ks[0], (B, S, D), dtype=jnp.float32), 'key': jax.random.normal(ks[1], (B, S, D), dtype=jnp.float32), 'value': jax.random.normal(ks[2], (B, S, D), dtype=jnp.float32), 'mask': jnp.ones((B, S), dtype=jnp.float32), 'Wq': g(ks[3], (H, D, DK)), 'Wk': g(ks[4], (H, D, DK)), 'Wv': g(ks[5], (H, D, DV)), 'Wo': g(ks[6], (H * DV, D)), 'W1': g(ks[7], (D, DFF)), 'b1': jnp.zeros((DFF,), dtype=jnp.float32), 'W2': g(ks[8], (DFF, D)), 'b2': jnp.zeros((D,), dtype=jnp.float32), 'gamma': jnp.ones((2,), dtype=jnp.float32), 'beta': jnp.zeros((2,), dtype=jnp.float32)}
    _L0_xattn_all = _L0_xattn_setup()
    _L0_xattn_in = {k: v for k, v in _L0_xattn_all.items() if k in ('Wq', 'Wk', 'Wv', 'Wo', 'W1', 'b1', 'W2', 'b2', 'gamma', 'beta')}
    del _L0_xattn_all

    def _L0_ffn_setup():
        import jax, jax.numpy as jnp
        import numpy as np
        B, S, D = (1, 256, 128)
        E, F = (16, 128)
        NG, TKG, K = (4, 2, 4)
        NSH = 2
        SCALE = 2.5
        STD = 0.02
        EPG = E // NG

        def _route(x_flat, router_w, bias):
            logits = x_flat.astype(jnp.float32) @ router_w.T
            scores = jax.nn.sigmoid(logits)
            s = scores + bias[None, :]
            sg = s.reshape(-1, NG, EPG)
            group_score = jax.lax.top_k(sg, 2)[0].sum(-1)
            gidx = jax.lax.top_k(group_score, TKG)[1]
            gmask = jnp.sum(jax.nn.one_hot(gidx, NG, dtype=jnp.float32), axis=1) > 0
            emask = jnp.repeat(gmask, EPG, axis=1)
            masked = jnp.where(emask, s, -1.0)
            topk_idx = jax.lax.top_k(masked, K)[1]
            tw = jnp.take_along_axis(scores, topk_idx, axis=1)
            tw = tw / (tw.sum(-1, keepdims=True) + 1e-20)
            tw = tw * SCALE
            return (topk_idx, tw)
        key = jax.random.key(seed)
        ks = jax.random.split(key, 8)
        return {'hidden_states': jax.random.normal(ks[0], (B, S, D), jnp.float32), 'router_w': jax.random.normal(ks[1], (E, D), jnp.float32) * STD, 'bias': jnp.zeros((E,), jnp.float32), 'gate_w': jax.random.normal(ks[2], (E, D, F), jnp.float32) * STD, 'up_w': jax.random.normal(ks[3], (E, D, F), jnp.float32) * STD, 'down_w': jax.random.normal(ks[4], (E, F, D), jnp.float32) * STD, 'sh_gate_w': jax.random.normal(ks[5], (D, NSH * F), jnp.float32) * STD, 'sh_up_w': jax.random.normal(ks[6], (D, NSH * F), jnp.float32) * STD, 'sh_down_w': jax.random.normal(ks[7], (NSH * F, D), jnp.float32) * STD}
    _L0_ffn_all = _L0_ffn_setup()
    _L0_ffn_in = {k: v for k, v in _L0_ffn_all.items() if k in ('router_w', 'bias', 'gate_w', 'up_w', 'down_w', 'sh_gate_w', 'sh_up_w', 'sh_down_w')}
    del _L0_ffn_all
    return {'x': x, 'ctx_1024': ctx_1024, 'mask_BxS2_ff1': mask_BxS2_ff1, 'L0_xattn_Wq': _L0_xattn_in['Wq'], 'L0_xattn_Wk': _L0_xattn_in['Wk'], 'L0_xattn_Wv': _L0_xattn_in['Wv'], 'L0_xattn_Wo': _L0_xattn_in['Wo'], 'L0_xattn_W1': _L0_xattn_in['W1'], 'L0_xattn_b1': _L0_xattn_in['b1'], 'L0_xattn_W2': _L0_xattn_in['W2'], 'L0_xattn_b2': _L0_xattn_in['b2'], 'L0_xattn_gamma': _L0_xattn_in['gamma'], 'L0_xattn_beta': _L0_xattn_in['beta'], 'L0_ffn_router_w': _L0_ffn_in['router_w'], 'L0_ffn_bias': _L0_ffn_in['bias'], 'L0_ffn_gate_w': _L0_ffn_in['gate_w'], 'L0_ffn_up_w': _L0_ffn_in['up_w'], 'L0_ffn_down_w': _L0_ffn_in['down_w'], 'L0_ffn_sh_gate_w': _L0_ffn_in['sh_gate_w'], 'L0_ffn_sh_up_w': _L0_ffn_in['sh_up_w'], 'L0_ffn_sh_down_w': _L0_ffn_in['sh_down_w']}

def reference(x, ctx_1024, mask_BxS2_ff1, L0_xattn_Wq, L0_xattn_Wk, L0_xattn_Wv, L0_xattn_Wo, L0_xattn_W1, L0_xattn_b1, L0_xattn_W2, L0_xattn_b2, L0_xattn_gamma, L0_xattn_beta, L0_ffn_router_w, L0_ffn_bias, L0_ffn_gate_w, L0_ffn_up_w, L0_ffn_down_w, L0_ffn_sh_gate_w, L0_ffn_sh_up_w, L0_ffn_sh_down_w):
    import jax
    import jax.numpy as jnp

    def _L0_xattn_ref(query, key, value, mask, Wq, Wk, Wv, Wo, W1, b1, W2, b2, gamma, beta):
        import jax, jax.numpy as jnp
        import numpy as np
        B, S, D = (4, 256, 128)
        H, DK, DV, DFF = (8, 128, 128, 256)
        MASK_VALUE = -1e+30
        EPS = 1e-14

        def _layernorm(x, g, b):
            mean = jnp.mean(x, axis=-1, keepdims=True)
            var = jnp.mean(jnp.square(x - mean), axis=-1, keepdims=True)
            return (x - mean) / jnp.sqrt(var + EPS) * g + b
        q = jnp.einsum('bsd,hdk->bhsk', query, Wq)
        k = jnp.einsum('btd,hdk->bhtk', key, Wk)
        v = jnp.einsum('btd,hdv->bhtv', value, Wv)
        A = jnp.einsum('bhsk,bhtk->bhst', q, k)
        m = mask[:, None, None, :]
        A = m * A + (1.0 - m) * MASK_VALUE
        A = jax.nn.softmax(A, axis=-1)
        o = jnp.einsum('bhst,bhtv->bshv', A, v).reshape(query.shape[0], query.shape[1], -1)
        proj = o @ Wo
        x = _layernorm(value + proj, gamma[0], beta[0])
        ffn = jax.nn.relu(x @ W1 + b1) @ W2 + b2
        x = _layernorm(x + ffn, gamma[1], beta[1])
        return x

    def _L0_ffn_ref(hidden_states, router_w, bias, gate_w, up_w, down_w, sh_gate_w, sh_up_w, sh_down_w):
        import jax, jax.numpy as jnp
        import numpy as np
        B, S, D = (1, 256, 128)
        E, F = (16, 128)
        NG, TKG, K = (4, 2, 4)
        NSH = 2
        SCALE = 2.5
        STD = 0.02
        EPG = E // NG

        def _route(x_flat, router_w, bias):
            logits = x_flat.astype(jnp.float32) @ router_w.T
            scores = jax.nn.sigmoid(logits)
            s = scores + bias[None, :]
            sg = s.reshape(-1, NG, EPG)
            group_score = jax.lax.top_k(sg, 2)[0].sum(-1)
            gidx = jax.lax.top_k(group_score, TKG)[1]
            gmask = jnp.sum(jax.nn.one_hot(gidx, NG, dtype=jnp.float32), axis=1) > 0
            emask = jnp.repeat(gmask, EPG, axis=1)
            masked = jnp.where(emask, s, -1.0)
            topk_idx = jax.lax.top_k(masked, K)[1]
            tw = jnp.take_along_axis(scores, topk_idx, axis=1)
            tw = tw / (tw.sum(-1, keepdims=True) + 1e-20)
            tw = tw * SCALE
            return (topk_idx, tw)
        x = hidden_states.reshape(-1, D)
        topk_idx, tw = _route(x, router_w, bias)
        combine = (jax.nn.one_hot(topk_idx, E, dtype=tw.dtype) * tw[..., None]).sum(1)
        h = jnp.einsum('td,edf->etf', x, gate_w)
        u = jnp.einsum('td,edf->etf', x, up_w)
        y = jnp.einsum('etf,efd->etd', jax.nn.silu(h) * u, down_w)
        routed = jnp.einsum('etd,te->td', y, combine)
        sh = jax.nn.silu(x @ sh_gate_w) * (x @ sh_up_w) @ sh_down_w
        return (routed + sh).reshape(hidden_states.shape)
    x = x + _L0_xattn_ref(_layernorm(x, axis=-1), ctx_1024, ctx_1024, mask_BxS2_ff1, L0_xattn_Wq, L0_xattn_Wk, L0_xattn_Wv, L0_xattn_Wo, L0_xattn_W1, L0_xattn_b1, L0_xattn_W2, L0_xattn_b2, L0_xattn_gamma, L0_xattn_beta)
    x = x + _L0_ffn_ref(_layernorm(x, axis=-1), L0_ffn_router_w, L0_ffn_bias, L0_ffn_gate_w, L0_ffn_up_w, L0_ffn_down_w, L0_ffn_sh_gate_w, L0_ffn_sh_up_w, L0_ffn_sh_down_w)
    return x

_drawn_inputs = setup_inputs


def setup_inputs(seed=0):
    import zlib

    import numpy as np

    out = dict(_drawn_inputs(seed))
    spreads = {'L0_xattn_b1': (0.0, 0.76),
     'L0_xattn_b2': (0.0, 0.1),
     'L0_xattn_gamma': (1.0, 0.2),
     'L0_xattn_beta': (0.0, 0.35),
     'L0_ffn_bias': (0.0, 0.8)}
    factors = {'L0_xattn_Wq': 5.081,
     'L0_xattn_Wk': 5.062,
     'L0_ffn_router_w': 8.0,
     'L0_ffn_gate_w': 8.0,
     'L0_ffn_up_w': 8.0,
     'L0_ffn_down_w': 8.0,
     'L0_ffn_sh_gate_w': 8.0,
     'L0_ffn_sh_up_w': 8.0,
     'L0_ffn_sh_down_w': 8.0}
    for name, (base, spread) in spreads.items():
        noise = np.random.default_rng([zlib.crc32(name.encode()), seed]).standard_normal(out[name].shape)
        drawn = base * np.exp(spread * noise) if base else spread * noise
        out[name] = jnp.asarray(drawn.astype(out[name].dtype))
    for name, factor in factors.items():
        out[name] = (out[name] * factor).astype(out[name].dtype)
    return out
```

```python
from contextlib import ExitStack

import concourse.bass as bass
import concourse.mybir as mybir
import numpy as np

F32 = mybir.dt.float32
F32R = mybir.dt.float32r
ALU = mybir.AluOpType
ACT = mybir.ActivationFunctionType
AX = mybir.AxisListType

P = 128
NB, SEQ = 32, 64
T = NB * SEQ
NT = T // P
CH = 4
TPC = NT // CH
CW = T // CH
BPC = NB // CH
NH = 8
HP = NH // 2
NF = 2
NSH = 2
NE = 16
NX = NSH + NE
NG, EPG = 4, 4
TOPK = 4
ROUTE_SCALE = 2.5
BIG = 1.0e30
EPS_IN, EPS_ATTN = 1e-5, 1e-14
LAG = 4
STEPS = 2 * CH


def build(nc, x, ctx_in, mask, wq, wk, wv, wo, w1, b1, w2, b2, gamma, beta,
          router_w, bias, gate_w, up_w, down_w, sh_gate, sh_up, sh_down, out):
    es = ExitStack()
    with es:
        es.enter_context(nc.allow_non_contiguous_dma(reason="two small vectors"))

        def sb(name, shape, dt=F32):
            return es.enter_context(nc.sbuf_tensor(name, shape, dt))

        def sem(name):
            return es.enter_context(nc.semaphore(name))

        x_all = sb("x_all", [P, NT, P])
        ctx_all = sb("ctx_all", [P, NT, P])
        mask_row = sb("mask_row", [P, T])
        mask_add = sb("mask_add", [P, CW])
        small_in = sb("small_in", [NE + NF, P])
        small_T = sb("small_T", [P, P])
        gam = sb("gam", [P, 2])
        bet = sb("bet", [P, 2])
        b2_row = sb("b2_row", [P, P])
        bias_row = sb("bias_row", [P, NE])
        wqk_in = sb("wqk_in", [P, 2, NH, P])
        wvo_in = sb("wvo_in", [P, 2, NH, P])
        wv_in, wo_in = wvo_in[:, 0], wvo_in[:, 1]
        w1_in = sb("w1_in", [P, NF * P])
        w2_in = sb("w2_in", [P, NF, P])
        w_exp = sb("w_exp", [P, NX, 3 * P])
        ident = sb("ident", [P, P])
        neg_half = sb("neg_half", [P, TPC])

        wT = sb("wT", [P, 3, NH, P])
        qk_hi, qk_lo = sb("qk_hi", [P, NH, P], F32R), sb("qk_lo", [P, NH, P], F32R)
        vo_hi, vo_lo = sb("vo_hi", [P, NH * P], F32R), sb("vo_lo", [P, NH * P], F32R)

        ctx_now = sb("ctx_now", [P, TPC, P])
        xnT_hi, xnT_lo = sb("xnT_hi", [P, CW], F32R), sb("xnT_lo", [P, CW], F32R)
        cT_hi, cT_lo = sb("cT_hi", [P, CW], F32R), sb("cT_lo", [P, CW], F32R)
        cT_m = sb("cT_m", [P, CW + SEQ])
        q_T = sb("q_T", [P, BPC, NH, SEQ])
        v_o = [sb(f"v_o{i}", [P, NH, P]) for i in range(2)]
        sc_m = [sb(f"sc_m{i}", [P, 2, HP, SEQ]) for i in range(2)]
        prob = [sb(f"prob{i}", [P, HP, 2, SEQ]) for i in range(2)]
        nmax = [sb(f"nmax{i}", [P, 2 * HP]) for i in range(2)]
        esum = [sb(f"esum{i}", [P, 2 * HP]) for i in range(2)]
        rsum = [sb(f"rsum{i}", [P, 2 * HP]) for i in range(2)]
        prob_T = [sb(f"prob_T{i}", [P, NH, 2, SEQ]) for i in range(2)]

        x1_b2 = sb("x1_b2", [P, TPC, P])
        x1_T = sb("x1_T", [P, CW])
        hid = sb("hid", [P, NF, CW])
        z = x1_b2
        xm_T = sb("xm_T", [P, CW])
        y = x2 = ctx_all
        x_beta = x_all
        mT_hi, mT_lo = sb("mT_hi", [P, T], F32R), sb("mT_lo", [P, T], F32R)
        logits = sb("logits", [P, NT, NE])

        cen = [sb(f"cen{i}", [P, TPC, P]) for i in range(4)]
        sqr = [sb(f"sqr{i}", [P, TPC, P]) for i in range(4)]
        xn, x1, xm = cen[0], cen[1], cen[3]
        tot = [sb(f"tot{i}", [P, TPC]) for i in range(4)]
        mean = [sb(f"mean{i}", [P, TPC]) for i in range(4)]
        vtot = [sb(f"vtot{i}", [P, TPC]) for i in range(4)]
        var = [sb(f"var{i}", [P, TPC]) for i in range(4)]
        rstd = [sb(f"rstd{i}", [P, TPC]) for i in range(4)]
        rstd_g = [sb(f"rstd_g{i}", [P, TPC]) for i in range(4)]

        we_hi = [sb(f"we_hi{i}", [P, 3 * P], F32R) for i in range(2)]
        we_lo = [sb(f"we_lo{i}", [P, 3 * P], F32R) for i in range(2)]
        comb = [wqk_in[:].rearrange("p a h k -> p (a h k)"), wvo_in[:].rearrange("p a h k -> p (a h k)")]
        wT_flat = wT[:].rearrange("p a h k -> p (a h k)").rearrange("p (n t) -> p n t", t=CW)
        silu, s_u, act = ([wT_flat[:, 2 * a + i, :] for i in range(2)] for a in range(3))
        act_hi = [w[:].rearrange("p h k -> p (h k)")[:, i * CW:(i + 1) * CW] for w in (qk_hi, qk_lo) for i in range(2)]
        act_lo = [w[:, i * CW:(i + 1) * CW] for w in (vo_hi, vo_lo) for i in range(2)]
        comb_dram = nc.dram_tensor("comb_dram", [2, P, P], F32, kind="Internal").ap()

        r_e = q_T[:].rearrange("p b h s -> p (b h s)")

        def route_tile(n, width=NE):
            return r_e[:, n * NT * NE:n * NT * NE + NT * width].rearrange("p (t e) -> p t e", e=width)

        score, biased, picked, m_eq, m_gt, m_pre, m_pre2, m_tmp, comb_w = (route_tile(n) for n in range(9))
        pair_sum = r_e[:, 9 * NT * NE:9 * NT * NE + NT * NG * 6].rearrange("p (t g n) -> p t g n", g=NG, n=6)
        pool3 = sc_m[0][:].rearrange("p a b c -> p (a b c)")
        g_score = pool3[:, 0:NT * NG].rearrange("p (t g) -> p t g", g=NG)
        g_keep = pool3[:, NT * NG:2 * NT * NG].rearrange("p (t g) -> p t g", g=NG)
        g_rank = pool3[:, 2 * NT * NG:3 * NT * NG].rearrange("p (t g) -> p t g", g=NG)
        gg_a = sc_m[1][:].rearrange("p a b c -> p (a b c)")[:, 0:NT * 16].rearrange("p (t g k) -> p t g k", g=NG, k=NG)
        gg_b = sc_m[1][:].rearrange("p a b c -> p (a b c)")[:, NT * 16:].rearrange("p (t g k) -> p t g k", g=NG, k=NG)
        lower = sb("lower", [P, NG, NG])
        top8 = sb("top8", [P, NT, 8])
        n_gt = sb("n_gt", [P, NT])
        w_sum = sb("w_sum", [P, NT])
        w_inv = sb("w_inv", [P, NT])
        comb_T = sb("comb_T", [P, 2, P])

        bank = [es.enter_context(nc.psum_tensor(f"bank{i}", [P, CW], F32)) for i in range(8)]
        work = bank[0:3]
        sc_bank = bank[3:5]
        t_bank, av_bank, post_bank = bank[5], bank[6], bank[7]
        acc = [bank[0], bank[1], bank[2], bank[6]]
        h_bank, u_bank = [bank[3], bank[5]], [bank[4], bank[7]]

        ld_x0, ld_x, ld_c0, ld_c = sem("ld_x0"), sem("ld_x"), sem("ld_c0"), sem("ld_c")
        ld_mask, ld_small, ld_vec = sem("ld_mask"), sem("ld_small"), sem("ld_vec")
        ld_wq, ld_wk, ld_wv, ld_wo, ld_ffn = sem("ld_wq"), sem("ld_wk"), sem("ld_wv"), sem("ld_wo"), sem("ld_ffn")
        ld_exp = sem("ld_exp")
        const_step, ident_done, zero_done = sem("const_step"), sem("ident_done"), sem("zero_done")
        small_zero = sem("small_zero")
        small_turned, small_done = sem("small_turned"), sem("small_done")
        mask_done = sem("mask_done")
        w_turned = sem("w_turned")
        wT_done = [sem(f"wT_done{i}") for i in range(3)]
        fold_done = sem("fold_done")
        fold_hi, fold_lo = sem("fold_hi"), sem("fold_lo")
        tot_ready = [sem(f"tot_ready{i}") for i in range(4)]
        mean_ready = [sem(f"mean_ready{i}") for i in range(4)]
        cen_ready = [sem(f"cen_ready{i}") for i in range(4)]
        sqr_ready = [sem(f"sqr_ready{i}") for i in range(4)]
        vtot_ready = [sem(f"vtot_ready{i}") for i in range(4)]
        var_ready = [sem(f"var_ready{i}") for i in range(4)]
        rstd_step = [sem(f"rstd_step{i}") for i in range(4)]
        rstd_ready = [sem(f"rstd_ready{i}") for i in range(4)]
        norm_ready = [sem(f"norm_ready{i}") for i in range(4)]
        ctx_now_ready = sem("ctx_now_ready")
        work_full = [sem(f"work_full{i}") for i in range(3)]
        work_free = [sem(f"work_free{i}") for i in range(3)]
        xnT_hi_ready, xnT_ready = sem("xnT_hi_ready"), sem("xnT_ready")
        cT_hi_ready, cT_lo_ready, cT_m_ready = sem("cT_hi_ready"), sem("cT_lo_ready"), sem("cT_m_ready")
        sc_full, sc_taken, max_ready = sem("sc_full"), sem("sc_taken"), sem("max_ready")
        sub_ready, exp_ready, sum_ready, rsum_ready = sem("sub_ready"), sem("exp_ready"), sem("sum_ready"), sem("rsum_ready")
        prob_ready, t_full, prob_T_ready = sem("prob_ready"), sem("t_full"), sem("prob_T_ready")
        av_full, y_ready = sem("av_full"), sem("y_ready")
        post_full, post_free = sem("post_full"), sem("post_free")
        x1_b2_ready, x_beta_ready = sem("x1_b2_ready"), sem("x_beta_ready")
        mT_hi_ready, xm_T_ready = sem("mT_hi_ready"), sem("xm_T_ready")
        exp_l_ready, route_step, route_done = sem("exp_l_ready"), sem("route_step"), sem("route_done")
        comb_turned, comb_T_ready, comb_stored = sem("comb_turned"), sem("comb_T_ready"), sem("comb_stored")
        ones_ready = sem("ones_ready")
        comb_loaded = [sem(f"comb_loaded{i}") for i in range(2)]
        gu_hi_ready, gu_lo_ready, dn_hi_ready, dn_lo_ready = sem("gu_hi_ready"), sem("gu_lo_ready"), sem("dn_hi_ready"), sem("dn_lo_ready")
        h_full, u_full, down_full = sem("h_full"), sem("u_full"), sem("down_full")
        silu_ready, s_u_ready, act_ready = sem("silu_ready"), sem("s_u_ready"), sem("act_ready")
        act_hi_ready, act_lo_ready = sem("act_hi_ready"), sem("act_lo_ready")
        acc_copied, out_turned, out_ready, stored = sem("acc_copied"), sem("out_turned"), sem("out_ready"), sem("stored")

        USES = 2 + NH + 2 * TPC
        per_slot = USES // 3
        assert USES % 3 == 0
        QUERY, VALUE = 2, 2 + NH

        def nth_use(c, k):
            return c * per_slot + (k // 3 + 1)

        def peeled(c):
            return isinstance(c, int) and c == 0

        POSTS = 6

        x_t = x.rearrange("b s d -> (b s) d").rearrange("(t p) d -> p t d", p=P)
        c_t = ctx_in.rearrange("b s d -> (b s) d").rearrange("(t p) d -> p t d", p=P)
        out_t = out.rearrange("b s d -> (b s) d").rearrange("(t p) d -> p t d", p=P)

        block = es.enter_context(nc.Block())

        @block.sync
        def _(sp):
            sp.dma_start(x_all[:, 0:TPC, :], x_t[:, 0:TPC, :]).then_inc(ld_x0, 16)
            sp.dma_start(ctx_all[:, 0:TPC, :], c_t[:, 0:TPC, :]).then_inc(ld_c0, 16)
            sp.dma_start(wv_in, wv.rearrange("h d v -> d h v")).then_inc(ld_wv, 16)
            sp.dma_start(wo_in, wo.rearrange("(h v) d -> v h d", v=P)).then_inc(ld_wo, 16)
            sp.dma_start(mask_row[:], mask.rearrange("b s -> (b s)").partition_broadcast(P)).then_inc(ld_mask, 16)
            sp.dma_start(x_all[:, TPC:, :], x_t[:, TPC:, :]).then_inc(ld_x, 16)
            sp.dma_start(ctx_all[:, TPC:, :], c_t[:, TPC:, :]).then_inc(ld_c, 16)
            sp.dma_start(w_exp[:, NSH:, 0:P], gate_w.rearrange("e d f -> d e f")).then_inc(ld_exp, 16)
            sp.dma_start(w_exp[:, NSH:, P:2 * P], up_w.rearrange("e d f -> d e f")).then_inc(ld_exp, 16)
            sp.dma_start(w_exp[:, NSH:, 2 * P:], down_w.rearrange("e f d -> f e d")).then_inc(ld_exp, 16)

            for half in range(2):
                sp.wait_ge(comb_T_ready, half + 1)
                sp.dma_start(comb_dram[half], comb_T[:, half, :]).then_inc(comb_stored, 16)
            sp.wait_ge(comb_stored, 32)
            by_expert = comb_dram.rearrange("a (t e) p -> e (a t) p", e=NE)
            with sp.Fori(1, NX // 2) as j:
                for i in range(2):
                    sp.wait_ge(act_ready, j * STEPS + ((i - 1) * CH))
                    sp.dma_start(comb[i].rearrange("p (a t) -> p a t", t=P),
                                 by_expert[bass.ds(j * 2 + (i - NSH), 1)].rearrange("e a t -> (e a) t")
                                 .partition_broadcast(P)).then_inc(comb_loaded[i], 16)
            for c in range(CH):
                sp.wait_ge(out_ready, c + 1)
                sp.dma_start(out_t[:, c * TPC:(c + 1) * TPC, :],
                             x2[:, c * TPC:(c + 1) * TPC, :]).then_inc(stored, 16)
            sp.wait_ge(stored, 16 * CH)

        @block.gpsimd
        def _(pool):
            def chunk_of(t, c):
                return t[:, bass.ts(c, TPC), :]

            def center(n, c, src):
                pool.wait_ge(ld_x0, 16)
                pool.wait_ge(mean_ready[n], c + 1)
                pool.tensor_tensor(cen[n][:], src if n == 2 else chunk_of(src, c), mean[n][:].unsqueeze(2).to_broadcast([P, TPC, P]),
                                   ALU.subtract).then_inc(cen_ready[n], 1)

            def inverse_root(n, c):
                pool.wait_ge(var_ready[n], c + 1)
                if n in (1, 2):
                    pool.tensor_tensor(rstd[n][:], var[n][:], neg_half[:], ALU.pow).then_inc(rstd_step[n], 1)
                    pool.wait_ge(rstd_step[n], c + 1)
                    pool.tensor_tensor(rstd_g[n][:], rstd[n][:], gam[:, n - 1:n].to_broadcast([P, TPC]),
                                       ALU.mult).then_inc(rstd_ready[n], 1)
                else:
                    pool.tensor_tensor(rstd[n][:], var[n][:], neg_half[:], ALU.pow).then_inc(rstd_ready[n], 1)

            def pre_center(c):
                center(0, c, x_all)

            def pre_root(c):
                inverse_root(0, c)

            def subtract_max(c, p):
                i = p % 2
                pool.wait_ge(max_ready, c * TPC + (p + 1))
                pool.tensor_tensor(sc_m[i][:], sc_m[i][:],
                                   nmax[i][:].rearrange("p (b h) -> p b h", h=HP).unsqueeze(3)
                                   .to_broadcast([P, 2, HP, SEQ]), ALU.add).then_inc(sub_ready, 1)

            def normalise_probs(c, p):
                i = p % 2
                pool.wait_ge(rsum_ready, c * TPC + (p + 1))
                if not (peeled(c) and p < 2):
                    pool.wait_ge(t_full, c * TPC + (p - 1))
                pool.tensor_tensor(prob[i][:].rearrange("p h b t -> p b h t"), sc_m[i][:],
                                   rsum[i][:].rearrange("p (b h) -> p b h", h=HP).unsqueeze(3)
                                   .to_broadcast([P, 2, HP, SEQ]), ALU.mult).then_inc(prob_ready, 1)

            def add_b2(c):
                pool.wait_ge(norm_ready[1], c + 1)
                pool.tensor_tensor(x1_b2[:], x1[:], b2_row[:].unsqueeze(1).to_broadcast([P, TPC, P]),
                                   ALU.add).then_inc(x1_b2_ready, 1)

            def add_beta(c):
                pool.wait_ge(ld_x0, 16)
                pool.wait_ge(norm_ready[0], c + 1)
                now = chunk_of(x_all, c)
                pool.tensor_tensor(now, now, bet[:, 1:2].unsqueeze(2).to_broadcast([P, TPC, P]),
                                   ALU.add).then_inc(x_beta_ready, 1)

            pool.memset(ident[:], 1.0).then_inc(const_step, 1)
            pool.wait_ge(const_step, 1)
            pool.affine_select(out=ident[:], in_=ident[:], compare_op=ALU.is_equal, fill=0.0, base=0,
                               pattern=[[1, P]], channel_multiplier=-1).then_inc(ident_done, 1)
            pool.memset(neg_half[:], -0.5).then_inc(const_step, 1)
            pool.wait_ge(const_step, 2)
            pool.wait_ge(ld_x0, 16)
            pre_center(0)
            pre_root(0)
            pool.memset(small_T[:], 0.0).then_inc(small_zero, 1)
            pool.memset(cT_m[:, CW:], 0.0)
            pool.memset(lower[:], 1.0).then_inc(const_step, 1)
            for i in range(2):
                z_last = pool.memset(prob_T[i][:], 0.0)
            z_last.then_inc(zero_done, 1)
            pool.wait_ge(const_step, 3)
            pool.affine_select(out=lower[:], in_=lower[:], compare_op=ALU.is_ge, fill=0.0, base=-1,
                               pattern=[[1, NG], [-1, NG]], channel_multiplier=0).then_inc(const_step, 1)
            pool.wait_ge(ld_vec, 64)

            def iteration(c, post, pre):
                if pre:
                    if peeled(c):
                        pool.wait_ge(ld_x, 16)
                if post:
                    center(1, c - 1, y)
                if pre:
                    pre_center(c + 1)
                if post:
                    inverse_root(1, c - 1)
                subtract_max(c, 0)
                if post:
                    add_b2(c - 1)
                    add_beta(c - 1)
                subtract_max(c, 1)
                normalise_probs(c, 0)
                if pre:
                    pre_root(c + 1)
                if post:
                    center(2, c - 1, z[:])
                    inverse_root(2, c - 1)
                subtract_max(c, 2)
                normalise_probs(c, 1)
                if post:
                    center(3, c - 1, x2)
                subtract_max(c, 3)
                normalise_probs(c, 2)
                if post:
                    inverse_root(3, c - 1)
                normalise_probs(c, 3)

            iteration(0, False, True)
            with pool.Fori(1, CH - 1) as c:
                iteration(c, True, True)
            iteration(CH - 1, True, False)
            last = CH - 1
            center(1, last, y)
            inverse_root(1, last)
            add_b2(last)
            add_beta(last)
            center(2, last, z[:])
            inverse_root(2, last)
            center(3, last, x2)
            inverse_root(3, last)

            def split_lo(part, e, slot):
                a, b = (0, 2 * P) if part == "gu" else (2 * P, 3 * P)
                hi, lo = (gu_hi_ready, gu_lo_ready) if part == "gu" else (dn_hi_ready, dn_lo_ready)
                pool.wait_ge(hi, e + 1)
                pool.tensor_tensor(we_lo[slot][:, a:b], w_exp[:, bass.ds(e, 1), a:b].rearrange("p e n -> p (e n)"),
                                   we_hi[slot][:, a:b].bitcast(F32), ALU.subtract).then_inc(lo, 1)

            def weigh(j, k):
                i, c = k // CH, k % CH
                n = j * STEPS + k
                pool.wait_ge(s_u_ready, n + 1)
                if not peeled(j) and c == 0:
                    pool.wait_ge(comb_loaded[i], j * 16)
                if not (peeled(j) and k < 2):
                    pool.wait_ge(act_lo_ready, n - 1)
                pool.tensor_tensor(act[k % 2], s_u[k % 2], comb[i][:, c * CW:(c + 1) * CW],
                                   ALU.mult).then_inc(act_ready, 1)

            def experts(j, last):
                for k in range(STEPS):
                    i, c = k // CH, k % CH
                    more = not (last and i == 1)
                    if c == 0 and more:
                        split_lo("gu", j * 2 + (i + 1), (i + 1) % 2)
                    weigh(j, k)
                    if c == CH - 1 and more:
                        split_lo("dn", j * 2 + (i + 1), (i + 1) % 2)

            pool.memset(comb[0], 1.0)
            pool.memset(comb[1], 1.0).then_inc(ones_ready, 1)
            pool.wait_ge(ones_ready, 1)
            split_lo("gu", 0, 0)
            split_lo("dn", 0, 0)
            experts(0, False)
            with pool.Fori(1, NX // 2 - 1) as j:
                experts(j, False)
            experts(NX // 2 - 1, True)

        @block.scalar
        def _(a):
            a.dma_start(wqk_in[:, 0], wq.rearrange("h d k -> d h k")).then_inc(ld_wq, 16)
            a.dma_start(wqk_in[:, 1], wk.rearrange("h d k -> d h k")).then_inc(ld_wk, 16)
            a.dma_start(small_in[0:NE, :], router_w).then_inc(ld_small, 16)
            a.dma_start(small_in[NE:NE + NF, :], b1.rearrange("(j f) -> j f", f=P)).then_inc(ld_small, 16)
            a.dma_start(gam[:], gamma.partition_broadcast(P)).then_inc(ld_vec, 16)
            a.dma_start(bet[:], beta.partition_broadcast(P)).then_inc(ld_vec, 16)
            a.dma_start(b2_row[:], b2.partition_broadcast(P)).then_inc(ld_vec, 16)
            a.dma_start(bias_row[:], bias.partition_broadcast(P)).then_inc(ld_vec, 16)
            a.dma_start(w1_in[:], w1).then_inc(ld_ffn, 16)
            a.dma_start(w2_in[:], w2.rearrange("(j f) d -> f j d", f=P)).then_inc(ld_ffn, 16)
            for i, w in enumerate((sh_gate, sh_up)):
                a.dma_start(w_exp[:, 0:NSH, i * P:(i + 1) * P], w.rearrange("d (e f) -> d e f", f=P)).then_inc(ld_exp, 16)
            a.dma_start(w_exp[:, 0:NSH, 2 * P:], sh_down.rearrange("(e f) d -> f e d", f=P)).then_inc(ld_exp, 16)

            def square(n, c):
                a.wait_ge(cen_ready[n], c + 1)
                a.activation(sqr[n][:], cen[n][:], ACT.Square).then_inc(sqr_ready[n], 1)

            def copy_ctx(c):
                if not peeled(c):
                    a.wait_ge(work_full[1], nth_use(c - 1, 1))
                a.copy(ctx_now[:], ctx_all[:, bass.ts(c, TPC), :]).then_inc(ctx_now_ready, 1)

            def xnT_high(c):
                a.wait_ge(work_full[0], nth_use(c, 0))
                if not peeled(c):
                    a.wait_ge(work_full[(VALUE - 1) % 3], nth_use(c - 1, VALUE - 1))
                a.copy(xnT_hi[:], work[0][:]).then_inc(xnT_hi_ready, 1)

            def cT_high(c):
                a.wait_ge(work_full[1], nth_use(c, 1))
                if not peeled(c):
                    a.wait_ge(work_full[(USES - 1) % 3], nth_use(c - 1, USES - 1))
                a.copy(cT_hi[:], work[1][:]).then_inc(cT_hi_ready, 1)

            def query(c, h):
                k = QUERY + h
                a.wait_ge(work_full[k % 3], nth_use(c, k))
                if h == 0 and not peeled(c):
                    a.wait_ge(sc_full, c * TPC)
                a.copy(q_T[:, :, h, :], work[k % 3][:].rearrange("p (b s) -> p b s", s=SEQ)
                       ).then_inc(work_free[k % 3], 1)

            def value(c, p):
                if not (peeled(c) and p < 2):
                    a.wait_ge(av_full, c * TPC + (p - 1))
                for j in range(2):
                    k = VALUE + 2 * p + j
                    a.wait_ge(work_full[k % 3], nth_use(c, k))
                    a.copy(v_o[p % 2][:, j * HP:(j + 1) * HP, :].rearrange("p h d -> p (h d)"),
                           work[k % 3][:]).then_inc(work_free[k % 3], 1)

            def exponent(c, p):
                a.wait_ge(sub_ready, c * TPC + (p + 1))
                a.activation(sc_m[p % 2][:], sc_m[p % 2][:], ACT.Exp).then_inc(exp_ready, 1)

            def spread(c, p):
                a.wait_ge(t_full, c * TPC + (p + 1))
                if not (peeled(c) and p < 2):
                    a.wait_ge(av_full, c * TPC + (p - 1))
                for s in range(2):
                    rows = slice(s * SEQ, (s + 1) * SEQ)
                    last = a.copy(prob_T[p % 2][rows, :, s, :],
                                  t_bank[rows, :].rearrange("p (h s) -> p h s", s=SEQ))
                last.then_inc(prob_T_ready, 1)

            def turn_x1(c):
                a.wait_ge(post_full, c * POSTS + 1)
                a.copy(x1_T[:], post_bank[:]).then_inc(post_free, 1)

            def hidden(c):
                for j in range(NF):
                    a.wait_ge(post_full, c * POSTS + (2 + j))
                    a.activation(hid[:, j, :], post_bank[:], ACT.Relu,
                                 bias=small_T[:, NE + j:NE + j + 1]).then_inc(post_free, 1)

            def xm_high(c):
                a.wait_ge(post_full, c * POSTS + 5)
                a.copy(mT_hi[:, bass.ts(c, CW)], post_bank[:]).then_inc(mT_hi_ready, 1)
                a.copy(xm_T[:], post_bank[:]).then_inc(xm_T_ready, 1)

            a.wait_ge(ld_c0, 16)
            copy_ctx(0)
            for i in range(3):
                a.wait_ge(w_turned, 2 * i + 1)
                a.copy(wT[:, i, 0:HP, :].rearrange("p h d -> p (h d)"), bank[2 * i][:]).then_inc(wT_done[i], 1)
            square(0, 0)
            a.wait_ge(small_turned, 1)
            a.wait_ge(small_zero, 1)
            a.copy(small_T[:, 0:NE + NF], bank[0][:, 0:NE + NF]).then_inc(small_done, 1)
            for i, (hi, half) in enumerate(((qk_hi, 0), (qk_hi, 1), (vo_hi, 0), (vo_hi, 1))):
                a.wait_ge(fold_done, i + 1)
                dst = hi[:, half * HP:(half + 1) * HP, :].rearrange("p h d -> p (h d)") if i < 2 else \
                    hi[:, half * CW:(half + 1) * CW]
                a.copy(dst, (bank[6], bank[7], bank[1], bank[2])[i][:]).then_inc(fold_hi, 1)
            a.wait_ge(small_done, 1)
            a.wait_ge(zero_done, 1)

            def iteration(c, post, pre):
                xnT_high(c)
                cT_high(c)
                if post:
                    spread(c - 1, TPC - 1)
                query(c, 0)
                query(c, 2)
                if post:
                    square(1, c - 1)
                query(c, 4)
                query(c, 6)
                if pre:
                    if peeled(c):
                        a.wait_ge(ld_c, 16)
                    copy_ctx(c + 1)
                    square(0, c + 1)
                value(c, 0)
                if post:
                    turn_x1(c - 1)
                    hidden(c - 1)
                exponent(c, 0)
                value(c, 1)
                exponent(c, 1)
                spread(c, 0)
                if post:
                    square(2, c - 1)
                value(c, 2)
                exponent(c, 2)
                spread(c, 1)
                value(c, 3)
                if post:
                    square(3, c - 1)
                exponent(c, 3)
                spread(c, 2)
                if post:
                    xm_high(c - 1)

            iteration(0, False, True)
            with a.Fori(1, CH - 1) as c:
                iteration(c, True, True)
            iteration(CH - 1, True, False)
            last = CH - 1
            spread(last, TPC - 1)
            square(1, last)
            turn_x1(last)
            hidden(last)
            square(2, last)
            square(3, last)
            xm_high(last)

            a.wait_ge(post_free, POSTS * CH)
            a.activation(score, logits[:], ACT.Exp, scale=-1.0).then_inc(exp_l_ready, 1)

            def split_hi(part, e, slot):
                a0, b0 = (0, 2 * P) if part == "gu" else (2 * P, 3 * P)
                hi = gu_hi_ready if part == "gu" else dn_hi_ready
                a.copy(we_hi[slot][:, a0:b0],
                       w_exp[:, bass.ds(e, 1), a0:b0].rearrange("p e n -> p (e n)")).then_inc(hi, 1)

            def gate(j, k):
                n = j * STEPS + k
                a.wait_ge(h_full, n + 1)
                if not (peeled(j) and k < 2):
                    a.wait_ge(s_u_ready, n - 1)
                a.activation(silu[k % 2], h_bank[k % 2][:], ACT.Silu).then_inc(silu_ready, 1)

            def act_high(j, k):
                n = j * STEPS + k
                a.wait_ge(act_ready, n + 1)
                if not (peeled(j) and k < 4):
                    a.wait_ge(down_full, n - 3)
                a.copy(act_hi[k % 4], act[k % 2]).then_inc(act_hi_ready, 1)

            def experts(j, last):
                for k in range(STEPS):
                    i, c = k // CH, k % CH
                    more = not (last and i == 1)
                    gate(j, k)
                    if not (peeled(j) and k == 0):
                        act_high(j, k - 1)
                    if c == 0 and more:
                        if not (peeled(j) and i == 0):
                            a.wait_ge(u_full, j * STEPS + i * CH)
                        split_hi("gu", j * 2 + (i + 1), (i + 1) % 2)
                    if c == CH - 1 and more:
                        if not (peeled(j) and i == 0):
                            a.wait_ge(down_full, j * STEPS + i * CH)
                        split_hi("dn", j * 2 + (i + 1), (i + 1) % 2)

            a.wait_ge(ld_exp, 6 * 16)
            split_hi("gu", 0, 0)
            split_hi("dn", 0, 0)
            experts(0, False)
            with a.Fori(1, NX // 2 - 1) as j:
                experts(j, False)
            experts(NX // 2 - 1, True)
            act_high(NX // 2, -1)
            for c in range(0, CH, 2):
                a.wait_ge(down_full, NX * CH - CH + c + 1)
                a.copy(q_T[:, 2 * c:2 * c + 2].rearrange("p b h s -> p (b h s)")[:, 0:CW], acc[c][:]).then_inc(acc_copied, 1)

        @block.vector
        def _(v):
            def mean_of(n, c, src):
                if n != 2:
                    src = src[:, bass.ts(c, TPC), :]
                v.tensor_reduce(tot[n][:], src, AX.X, ALU.add).then_inc(tot_ready[n], 1)
                v.wait_ge(tot_ready[n], c + 1)
                v.tensor_scalar(mean[n][:], tot[n][:], 1.0 / P, None, ALU.mult).then_inc(mean_ready[n], 1)

            def variance(n, c):
                v.wait_ge(sqr_ready[n], c + 1)
                v.tensor_reduce(vtot[n][:], sqr[n][:], AX.X, ALU.add).then_inc(vtot_ready[n], 1)
                v.wait_ge(vtot_ready[n], c + 1)
                v.tensor_scalar(var[n][:], vtot[n][:], 1.0 / P, EPS_ATTN if n in (1, 2) else EPS_IN,
                                ALU.mult, ALU.add).then_inc(var_ready[n], 1)

            def norm_plain(n, c, dst):
                v.wait_ge(rstd_ready[n], c + 1)
                for t in range(TPC):
                    last = v.tensor_scalar(dst[:, t, :], cen[n][:, t, :], rstd[n][:, t:t + 1], None, ALU.mult)
                last.then_inc(norm_ready[n], 1)

            def norm_input(c):
                norm_plain(0, c, xn)

            def norm_attn(c):
                v.wait_ge(rstd_ready[1], c + 1)
                for t in range(TPC):
                    last = v.tensor_scalar(x1[:, t, :], cen[1][:, t, :], rstd_g[1][:, t:t + 1], bet[:, 0:1],
                                           ALU.mult, ALU.add)
                last.then_inc(norm_ready[1], 1)

            def norm_ffn(c):
                v.wait_ge(rstd_ready[2], c + 1)
                v.wait_ge(x_beta_ready, c + 1)
                for t in range(TPC):
                    last = v.scalar_tensor_tensor(x2[:, bass.ds(c * TPC + t, 1), :].rearrange("p o d -> p (o d)"),
                                                  cen[2][:, t, :], rstd_g[2][:, t:t + 1],
                                                  x_beta[:, bass.ds(c * TPC + t, 1), :].rearrange("p o d -> p (o d)"),
                                                  ALU.mult, ALU.add)
                last.then_inc(norm_ready[2], 1)

            def xnT_low(c):
                v.wait_ge(xnT_hi_ready, c + 1)
                v.tensor_tensor(xnT_lo[:], work[0][:], xnT_hi[:].bitcast(F32), ALU.subtract).then_inc(work_free[0], 1)

            def cT_low(c):
                v.wait_ge(cT_hi_ready, c + 1)
                v.tensor_tensor(cT_lo[:], work[1][:], cT_hi[:].bitcast(F32), ALU.subtract).then_inc(cT_lo_ready, 1)
                if not peeled(c):
                    v.wait_ge(sc_full, c * TPC)
                v.tensor_tensor(cT_m[:, 0:CW], work[1][:], mask_row[:, bass.ts(c, CW)],
                                ALU.mult).then_inc(work_free[1], 1)
                v.tensor_scalar(mask_add[:], mask_row[:, bass.ts(c, CW)], -1.0, BIG, ALU.add,
                                ALU.mult).then_inc(mask_done, 1)

            def query(c, h):
                k = QUERY + h
                v.wait_ge(work_full[k % 3], nth_use(c, k))
                v.tensor_copy(q_T[:, :, h, :], work[k % 3][:].rearrange("p (b s) -> p b s", s=SEQ)
                              ).then_inc(work_free[k % 3], 1)

            def mask_and_max(c, p):
                i = p % 2
                v.wait_ge(sc_full, c * TPC + (p + 1))
                v.wait_ge(mask_done, c + 1)
                for s in range(2):
                    last = v.tensor_tensor(
                        sc_m[i][:, s], sc_bank[s][:].rearrange("p (h t) -> p h t", t=P)[:, :, 0:SEQ],
                        mask_add[:, (2 * p + s) * SEQ:(2 * p + s + 1) * SEQ].unsqueeze(1)
                        .to_broadcast([P, HP, SEQ]), ALU.add)
                last.then_inc(sc_taken, 1)
                v.wait_ge(sc_taken, c * TPC + (p + 1))
                v.tensor_reduce(nmax[i][:].rearrange("p (b h) -> p b h", h=HP), sc_m[i][:], AX.X, ALU.max,
                                negate=True).then_inc(max_ready, 1)

            def sum_of_exp(c, p):
                i = p % 2
                v.wait_ge(exp_ready, c * TPC + (p + 1))
                v.tensor_reduce(esum[i][:].rearrange("p (b h) -> p b h", h=HP), sc_m[i][:], AX.X,
                                ALU.add).then_inc(sum_ready, 1)
                v.wait_ge(sum_ready, c * TPC + (p + 1))
                v.reciprocal(rsum[i][:], esum[i][:]).then_inc(rsum_ready, 1)

            def add_ctx(c, p):
                v.wait_ge(av_full, c * TPC + (p + 1))
                tile = y[:, bass.ds(c * TPC + p, 1), :].rearrange("p o d -> p (o d)")
                v.tensor_tensor(tile, av_bank[:, 0:P], tile, ALU.add).then_inc(y_ready, 1)

            def add_ffn(c):
                v.wait_ge(post_full, c * POSTS + 4)
                v.wait_ge(x1_b2_ready, c + 1)
                v.tensor_tensor(z[:], post_bank[:].rearrange("p (t d) -> p t d", d=P), x1_b2[:],
                                ALU.add).then_inc(post_free, 1)

            def xm_low(c):
                v.wait_ge(mT_hi_ready, c + 1)
                v.wait_ge(xm_T_ready, c + 1)
                v.tensor_tensor(mT_lo[:, bass.ts(c, CW)], post_bank[:], mT_hi[:, bass.ts(c, CW)].bitcast(F32),
                                ALU.subtract).then_inc(post_free, 1)
                v.wait_ge(post_full, c * POSTS + 6)
                v.tensor_copy(logits[:, bass.ts(c, TPC), :],
                              post_bank[:].rearrange("p (t n) -> p t n", n=P)[:, :, 0:NE]).then_inc(post_free, 1)

            v.wait_ge(ld_x0, 16)
            mean_of(0, 0, x_all)
            for i in range(2):
                v.wait_ge(w_turned, 2 * i + 2)
                v.tensor_copy(wT[:, i, HP:, :].rearrange("p h d -> p (h d)"), bank[2 * i + 1][:]).then_inc(wT_done[i], 1)
            variance(0, 0)
            v.wait_ge(w_turned, 6)
            v.tensor_copy(wT[:, 2, HP:, :].rearrange("p h d -> p (h d)"), bank[5][:]).then_inc(wT_done[2], 1)
            v.wait_ge(const_step, 2)
            norm_input(0)
            for i, (hi, lo, half) in enumerate(((qk_hi, qk_lo, 0), (qk_hi, qk_lo, 1), (vo_hi, vo_lo, 0), (vo_hi, vo_lo, 1))):
                v.wait_ge(fold_hi, i + 1)
                dst, src = (w[:, half * HP:(half + 1) * HP, :].rearrange("p h d -> p (h d)") if i < 2 else
                            w[:, half * CW:(half + 1) * CW] for w in (lo, hi))
                v.tensor_tensor(dst, (bank[6], bank[7], bank[1], bank[2])[i][:], src.bitcast(F32),
                                ALU.subtract).then_inc(fold_lo, 1)
            v.wait_ge(ld_mask, 16)
            v.wait_ge(ld_c0, 16)

            def iteration(c, post, pre):
                xnT_low(c)
                cT_low(c)
                if post:
                    add_ctx(c - 1, TPC - 1)
                    v.wait_ge(ld_x0, 16)
                    v.wait_ge(y_ready, c * TPC)
                    mean_of(1, c - 1, y)
                query(c, 1)
                query(c, 3)
                if post:
                    variance(1, c - 1)
                query(c, 5)
                query(c, 7)
                if pre:
                    if peeled(c):
                        v.wait_ge(ld_x, 16)
                        v.wait_ge(ld_c, 16)
                    mean_of(0, c + 1, x_all)
                if post:
                    norm_attn(c - 1)
                mask_and_max(c, 0)
                mask_and_max(c, 1)
                if pre:
                    variance(0, c + 1)
                sum_of_exp(c, 0)
                if post:
                    add_ffn(c - 1)
                    v.wait_ge(post_free, (c - 1) * POSTS + 4)
                    mean_of(2, c - 1, z[:])
                sum_of_exp(c, 1)
                mask_and_max(c, 2)
                add_ctx(c, 0)
                if post:
                    variance(2, c - 1)
                if pre:
                    norm_input(c + 1)
                if post:
                    norm_ffn(c - 1)
                    v.wait_ge(ld_x0, 16)
                    v.wait_ge(norm_ready[2], c)
                    mean_of(3, c - 1, x2)
                mask_and_max(c, 3)
                sum_of_exp(c, 2)
                add_ctx(c, 1)
                if post:
                    variance(3, c - 1)
                sum_of_exp(c, 3)
                if post:
                    norm_plain(3, c - 1, xm)
                add_ctx(c, 2)
                if post:
                    xm_low(c - 1)

            iteration(0, False, True)
            with v.Fori(1, CH - 1) as c:
                iteration(c, True, True)
            iteration(CH - 1, True, False)
            last = CH - 1
            add_ctx(last, TPC - 1)
            v.wait_ge(y_ready, CH * TPC)
            mean_of(1, last, y)
            variance(1, last)
            norm_attn(last)
            add_ffn(last)
            v.wait_ge(post_free, last * POSTS + 4)
            mean_of(2, last, z[:])
            variance(2, last)
            norm_ffn(last)
            v.wait_ge(norm_ready[2], CH)
            mean_of(3, last, x2)
            variance(3, last)
            norm_plain(3, last, xm)
            xm_low(last)

            steps = [0]

            def done(ins):
                steps[0] += 1
                ins.then_inc(route_step, 1)
                v.wait_ge(route_step, steps[0])

            def by_token(t, n):
                return t[:].unsqueeze(2).to_broadcast([P, NT, n])

            def sigmoid_and_groups():
                v.wait_ge(exp_l_ready, 1)
                v.wait_ge(const_step, 4)
                done(v.tensor_scalar(m_tmp, score, 1.0, None, ALU.add))
                done(v.reciprocal(score, m_tmp))
                done(v.tensor_tensor(biased, score, bias_row[:].unsqueeze(1).to_broadcast([P, NT, NE]), ALU.add))
                s4 = biased.rearrange("p t (g n) -> p t g n", n=EPG)
                v.tensor_tensor(pair_sum[:, :, :, 0:3], s4[:, :, :, 0:3], s4[:, :, :, 1:4], ALU.add)
                v.tensor_tensor(pair_sum[:, :, :, 3:5], s4[:, :, :, 0:2], s4[:, :, :, 2:4], ALU.add)
                done(v.tensor_tensor(pair_sum[:, :, :, 5:6], s4[:, :, :, 0:1], s4[:, :, :, 3:4], ALU.add))
                done(v.tensor_reduce(g_score, pair_sum, AX.X, ALU.max))

            def keep_groups():
                mine = g_score.unsqueeze(3).to_broadcast([P, NT, NG, NG])
                other = g_score.unsqueeze(2).to_broadcast([P, NT, NG, NG])
                before = lower[:].unsqueeze(1).to_broadcast([P, NT, NG, NG])
                done(v.tensor_tensor(gg_a, other, mine, ALU.is_equal))
                done(v.tensor_tensor(gg_b, gg_a, before, ALU.mult))
                done(v.tensor_tensor(gg_a, other, mine, ALU.is_gt))
                done(v.tensor_tensor(gg_a, gg_a, gg_b, ALU.add))
                done(v.tensor_reduce(g_rank, gg_a, AX.X, ALU.add))
                done(v.tensor_scalar(g_keep, g_rank, 1.5, None, ALU.is_lt))
                done(v.tensor_scalar(g_rank, g_keep, -1.0, None, ALU.add))
                keep = g_keep.unsqueeze(3).to_broadcast([P, NT, NG, EPG])
                less = g_rank.unsqueeze(3).to_broadcast([P, NT, NG, EPG])
                done(v.tensor_tensor(m_tmp.rearrange("p t (g n) -> p t g n", n=EPG),
                                     biased.rearrange("p t (g n) -> p t g n", n=EPG), keep, ALU.mult))
                done(v.tensor_tensor(picked.rearrange("p t (g n) -> p t g n", n=EPG),
                                     m_tmp.rearrange("p t (g n) -> p t g n", n=EPG), less, ALU.add))

            def keep_experts():
                for t in range(NT):
                    last = v.max(top8[:, t, :], picked[:, t, :])
                done(last)
                fourth = top8[:, :, TOPK - 1:TOPK].to_broadcast([P, NT, NE])
                done(v.tensor_tensor(m_gt, picked, fourth, ALU.is_gt))
                done(v.tensor_tensor(m_eq, picked, fourth, ALU.is_equal))
                done(v.tensor_reduce(n_gt[:], m_gt, AX.X, ALU.add))
                src, dst = m_eq, m_pre
                for step in (1, 2, 4, 8):
                    v.tensor_copy(dst[:, :, 0:step], src[:, :, 0:step])
                    done(v.tensor_tensor(dst[:, :, step:], src[:, :, step:], src[:, :, 0:NE - step], ALU.add))
                    src, dst = dst, (m_pre2 if dst is m_pre else m_pre)
                done(v.tensor_tensor(m_tmp, src, by_token(n_gt, NE), ALU.add))
                done(v.tensor_scalar(m_tmp, m_tmp, TOPK + 0.5, None, ALU.is_lt))
                done(v.tensor_tensor(m_tmp, m_tmp, m_eq, ALU.mult))
                done(v.tensor_tensor(m_tmp, m_tmp, m_gt, ALU.add))

            def combine():
                done(v.tensor_tensor(m_gt, m_tmp, score, ALU.mult))
                done(v.tensor_reduce(w_sum[:], m_gt, AX.X, ALU.add))
                done(v.tensor_scalar(w_sum[:], w_sum[:], 1e-20, None, ALU.add))
                done(v.reciprocal(w_inv[:], w_sum[:]))
                done(v.tensor_tensor(m_tmp, m_gt, by_token(w_inv, NE), ALU.mult))
                v.tensor_scalar(comb_w, m_tmp, ROUTE_SCALE, None, ALU.mult).then_inc(route_done, 1)

            sigmoid_and_groups()
            keep_groups()
            keep_experts()
            combine()
            for half in range(2):
                v.wait_ge(comb_turned, half + 1)
                v.tensor_copy(comb_T[:, half, :], acc[half][:, 0:P]).then_inc(comb_T_ready, 1)

            def gate_up(j, k):
                n = j * STEPS + k
                v.wait_ge(silu_ready, n + 1)
                v.wait_ge(u_full, n + 1)
                if not (peeled(j) and k < 2):
                    v.wait_ge(act_ready, n - 1)
                v.tensor_tensor(s_u[k % 2], u_bank[k % 2][:], silu[k % 2], ALU.mult).then_inc(s_u_ready, 1)

            def act_low(j, k):
                n = j * STEPS + k
                v.wait_ge(act_hi_ready, n + 1)
                v.tensor_tensor(act_lo[k % 4], act[k % 2], act_hi[k % 4].bitcast(F32),
                                ALU.subtract).then_inc(act_lo_ready, 1)

            def experts(j):
                for k in range(STEPS):
                    gate_up(j, k)
                    if not (peeled(j) and k == 0):
                        act_low(j, k - 1)

            experts(0)
            with v.Fori(1, NX // 2) as j:
                experts(j)
            act_low(NX // 2, -1)
            for c in range(1, CH, 2):
                v.wait_ge(down_full, NX * CH - CH + c + 1)
                v.tensor_copy(q_T[:, 2 * c:2 * c + 2].rearrange("p b h s -> p (b h s)")[:, 0:CW], acc[c][:]).then_inc(acc_copied, 1)
            for c in range(CH):
                v.wait_ge(out_turned, c + 1)
                v.tensor_tensor(x2[:, c * TPC:(c + 1) * TPC, :], (h_bank + u_bank)[c][:].rearrange("p (t d) -> p t d", d=P),
                                x2[:, c * TPC:(c + 1) * TPC, :], ALU.add).then_inc(out_ready, 1)

        @block.tensor
        def _(pe):
            def three(dst, w_hi, w_lo, m_hi, m_lo, start, stop):
                pe.matmul(dst, w_hi, m_hi, start=start, stop=False)
                pe.matmul(dst, w_hi, m_lo, start=False, stop=False)
                return pe.matmul(dst, w_lo, m_hi, start=False, stop=stop)

            def work_bank(c, k):
                if not (peeled(c) and k < 3):
                    pe.wait_ge(work_free[k % 3], nth_use(c, k) - 1)
                return work[k % 3]

            def turn_inputs(c):
                w = work_bank(c, 0)
                pe.wait_ge(norm_ready[0], c + 1)
                for t in range(TPC):
                    last = pe.transpose(w[:, t * P:(t + 1) * P], xn[:, t, :], ident[:])
                last.then_inc(work_full[0], 1)
                w = work_bank(c, 1)
                pe.wait_ge(ctx_now_ready, c + 1)
                for t in range(TPC):
                    last = pe.transpose(w[:, t * P:(t + 1) * P], ctx_now[:, t, :], ident[:])
                last.then_inc(work_full[1], 1)

            def queries(c):
                pe.wait_ge(work_free[0], nth_use(c, 0))
                for h in range(NH):
                    k = QUERY + h
                    w = work_bank(c, k)
                    three(w[:], qk_hi[:, h, :], qk_lo[:, h, :], xnT_hi[:], xnT_lo[:], True, True
                          ).then_inc(work_full[k % 3], 1)

            def values(c, p):
                if p == 0:
                    pe.wait_ge(cT_lo_ready, c + 1)
                tok = slice(p * P, (p + 1) * P)
                for j in range(2):
                    k = VALUE + 2 * p + j
                    w = work_bank(c, k)
                    cols = slice(j * CW, (j + 1) * CW)
                    three_moving(w[:], cT_hi[:, tok], cT_lo[:, tok], vo_hi[:, cols], vo_lo[:, cols]
                                 ).then_inc(work_full[k % 3], 1)

            def three_moving(dst, w_hi, w_lo, m_hi, m_lo):
                return three(dst, w_hi, w_lo, m_hi, m_lo, True, True)

            def scores(c, p):
                if p == 0:
                    for k in range(VALUE - 3, VALUE):
                        pe.wait_ge(work_free[k % 3], nth_use(c, k))
                    pe.wait_ge(work_free[1], nth_use(c, 1))
                if not (peeled(c) and p == 0):
                    pe.wait_ge(sc_taken, c * TPC + p)
                for s in range(2):
                    b = 2 * p + s
                    for hp in range(HP):
                        last = pe.matmul(sc_bank[s][:, hp * P:(hp + 1) * P],
                                         q_T[:, b, 2 * hp:2 * hp + 2, :].rearrange("p h s -> p (h s)"),
                                         cT_m[:, b * SEQ:b * SEQ + P], start=True, stop=True)
                last.then_inc(sc_full, 1)

            def turn_probs(c, p):
                pe.wait_ge(prob_ready, c * TPC + (p + 1))
                if not (peeled(c) and p == 0):
                    pe.wait_ge(prob_T_ready, c * TPC + p)
                for hp in range(HP):
                    last = pe.transpose(t_bank[:, hp * P:(hp + 1) * P],
                                        prob[p % 2][:, hp, :, :].rearrange("p b t -> p (b t)"), ident[:])
                last.then_inc(t_full, 1)

            def attend(c, p):
                pe.wait_ge(prob_T_ready, c * TPC + (p + 1))
                for j in range(2):
                    k = VALUE + 2 * p + j
                    pe.wait_ge(work_free[k % 3], nth_use(c, k))
                if not (peeled(c) and p == 0):
                    pe.wait_ge(y_ready, c * TPC + p)
                for h in range(NH):
                    last = pe.matmul(av_bank[:, 0:P], prob_T[p % 2][:, h, :, :].rearrange("p b s -> p (b s)"),
                                     v_o[p % 2][:, h, :], start=(h == 0), stop=(h == NH - 1))
                last.then_inc(av_full, 1)

            def post_bank_for(c, k):
                pe.wait_ge(post_free, c * POSTS + k)

            def ffn_up(c):
                pe.wait_ge(norm_ready[1], c + 1)
                for t in range(TPC):
                    last = pe.transpose(post_bank[:, t * P:(t + 1) * P], x1[:, t, :], ident[:])
                last.then_inc(post_full, 1)
                for j in range(NF):
                    post_bank_for(c, 1 + j)
                    pe.matmul(post_bank[:], w1_in[:, j * P:(j + 1) * P], x1_T[:],
                              start=True, stop=True).then_inc(post_full, 1)

            def ffn_down(c):
                post_bank_for(c, 3)
                for t in range(TPC):
                    for j in range(NF):
                        last = pe.matmul(post_bank[:, t * P:(t + 1) * P], hid[:, j, t * P:(t + 1) * P],
                                         w2_in[:, j, :], start=(j == 0), stop=(j == NF - 1))
                last.then_inc(post_full, 1)

            def turn_xm(c):
                post_bank_for(c, 4)
                pe.wait_ge(norm_ready[3], c + 1)
                for t in range(TPC):
                    last = pe.transpose(post_bank[:, t * P:(t + 1) * P], xm[:, t, :], ident[:])
                last.then_inc(post_full, 1)

            def route(c):
                post_bank_for(c, 5)
                pe.wait_ge(xm_T_ready, c + 1)
                for t in range(TPC):
                    last = pe.matmul(post_bank[:, t * P:(t + 1) * P], xm_T[:, t * P:(t + 1) * P], small_T[:],
                                     start=True, stop=True)
                last.then_inc(post_full, 1)

            pe.wait_ge(ident_done, 1)
            for i, ready in enumerate((ld_wq, ld_wk, ld_wv)):
                pe.wait_ge(ready, 16)
                for half in range(2):
                    for h in range(HP):
                        src = wqk_in[:, i, half * HP + h, :] if i < 2 else wv_in[:, half * HP + h, :]
                        last = pe.transpose(bank[2 * i + half][:, h * P:(h + 1) * P], src, ident[:])
                    last.then_inc(w_turned, 1)
            for i in range(2):
                pe.wait_ge(wT_done[i], 2)
            for half in range(2):
                for h in range(HP):
                    hh = half * HP + h
                    last = pe.matmul(bank[6 + half][:, h * P:(h + 1) * P], wT[:, 0, hh, :], wT[:, 1, hh, :],
                                     start=True, stop=True)
                last.then_inc(fold_done, 1)
            pe.wait_ge(ld_small, 32)
            pe.transpose(bank[0][:, 0:NE + NF], small_in[:], ident[0:NE + NF, 0:NE + NF]).then_inc(small_turned, 1)
            pe.wait_ge(wT_done[2], 2)
            pe.wait_ge(ld_wo, 16)
            for half in range(2):
                for h in range(HP):
                    hh = half * HP + h
                    last = pe.matmul(bank[1 + half][:, h * P:(h + 1) * P], wT[:, 2, hh, :], wo_in[:, hh, :],
                                     start=True, stop=True)
                last.then_inc(fold_done, 1)
            pe.wait_ge(small_done, 1)
            pe.wait_ge(fold_lo, 4)
            pe.wait_ge(zero_done, 1)
            pe.wait_ge(ld_ffn, 32)

            def iteration(c, post):
                turn_inputs(c)
                if post:
                    turn_probs(c - 1, TPC - 1)
                    attend(c - 1, TPC - 1)
                queries(c)
                values(c, 0)
                scores(c, 0)
                if post:
                    ffn_up(c - 1)
                values(c, 1)
                scores(c, 1)
                if post:
                    ffn_down(c - 1)
                turn_probs(c, 0)
                attend(c, 0)
                values(c, 2)
                scores(c, 2)
                turn_probs(c, 1)
                attend(c, 1)
                values(c, 3)
                scores(c, 3)
                turn_probs(c, 2)
                attend(c, 2)
                if post:
                    turn_xm(c - 1)
                    route(c - 1)

            iteration(0, False)
            with pe.Fori(1, CH) as c:
                iteration(c, True)
            last_c = CH - 1
            turn_probs(last_c, TPC - 1)
            attend(last_c, TPC - 1)
            ffn_up(last_c)
            ffn_down(last_c)
            turn_xm(last_c)
            route(last_c)
            pe.wait_ge(post_free, POSTS * CH)
            pe.wait_ge(y_ready, CH * TPC)

            def turn_combine():
                pe.wait_ge(route_done, 1)
                for half in range(2):
                    pe.transpose(acc[half][:, 0:P], comb_w.rearrange("p t e -> p (t e)")[:, half * P:(half + 1) * P],
                                 ident[:]).then_inc(comb_turned, 1)
                pe.wait_ge(comb_T_ready, 2)

            def up(j, k):
                n = j * STEPS + k
                i, c = k // CH, k % CH
                if c == 0:
                    pe.wait_ge(gu_lo_ready, j * 2 + (i + 1))
                cols = slice(c * CW, (c + 1) * CW)
                if not (peeled(j) and k < 2):
                    pe.wait_ge(silu_ready, n - 1)
                three(h_bank[k % 2][:], we_hi[i][:, 0:P], we_lo[i][:, 0:P], mT_hi[:, cols], mT_lo[:, cols],
                      True, True).then_inc(h_full, 1)
                if not (peeled(j) and k < 2):
                    pe.wait_ge(s_u_ready, n - 1)
                three(u_bank[k % 2][:], we_hi[i][:, P:2 * P], we_lo[i][:, P:2 * P], mT_hi[:, cols], mT_lo[:, cols],
                      True, True).then_inc(u_full, 1)

            def down(j, k, start=False, stop=False):
                n = j * STEPS + k
                i, c = (k // CH) % 2, k % CH
                if c == 0:
                    pe.wait_ge(dn_lo_ready, j * 2 + (k // CH + 1))
                pe.wait_ge(act_lo_ready, n + 1)
                three(acc[c][:], we_hi[i][:, 2 * P:], we_lo[i][:, 2 * P:], act_hi[k % 4], act_lo[k % 4],
                      start, stop).then_inc(down_full, 1)

            def experts(j):
                for k in range(STEPS):
                    up(j, k)
                    if not (peeled(j) and k < LAG):
                        down(j, k - LAG, start=(peeled(j) and k - LAG < CH))

            turn_combine()
            experts(0)
            with pe.Fori(1, NX // 2) as j:
                experts(j)
            for k in range(-LAG, 0):
                down(NX // 2, k, stop=True)
            for c in range(CH):
                pe.wait_ge(acc_copied, CH)
                dst = (h_bank + u_bank)[c]
                src = q_T[:, 2 * c:2 * c + 2].rearrange("p b h s -> p (b h s)")
                for t in range(TPC):
                    last = pe.transpose(dst[:, t * P:(t + 1) * P], src[:, t * P:(t + 1) * P], ident[:])
                last.then_inc(out_turned, 1)


_INS = ['x', 'ctx_1024', 'mask_BxS2_ff1', 'L0_xattn_Wq', 'L0_xattn_Wk', 'L0_xattn_Wv', 'L0_xattn_Wo', 'L0_xattn_W1',
        'L0_xattn_b1', 'L0_xattn_W2', 'L0_xattn_b2', 'L0_xattn_gamma', 'L0_xattn_beta', 'L0_ffn_router_w',
        'L0_ffn_bias', 'L0_ffn_gate_w', 'L0_ffn_up_w', 'L0_ffn_down_w', 'L0_ffn_sh_gate_w', 'L0_ffn_sh_up_w',
        'L0_ffn_sh_down_w']


def kernel(**inputs):
    import concourse.bacc as bacc
    from concourse.bass_utils import run_bass_kernel_spmd

    nc = bacc.Bacc("TRN2", target_bir_lowering=False, num_devices=1)
    arrays, args = {}, []
    for name in _INS:
        a = np.ascontiguousarray(inputs[name])
        arrays[f"in_{name}"] = a
        args.append(nc.dram_tensor(f"in_{name}", a.shape, mybir.dt.from_np(a.dtype), kind="ExternalInput").ap())
    args.append(nc.dram_tensor("out_x", (NB, SEQ, P), F32, kind="ExternalOutput").ap())
    build(nc, *args)
    r = run_bass_kernel_spmd(nc, [arrays], core_ids=[0])
    return r.results[0]["out_x"]
```

```python
from contextlib import ExitStack

import concourse.bass as bass
import concourse.mybir as mybir
import numpy as np

F32 = mybir.dt.float32
F32R = mybir.dt.float32r
ALU = mybir.AluOpType
ACT = mybir.ActivationFunctionType
AX = mybir.AxisListType

P = 128
NB, SEQ = 32, 64
T = NB * SEQ
NT = T // P
CH = 4
TPC = NT // CH
CW = T // CH
BPC = NB // CH
NH = 8
HP = NH // 2
NF = 2
NSH = 2
NE = 16
NX = NSH + NE
NG, EPG = 4, 4
TOPK = 4
ROUTE_SCALE = 2.5
BIG = 1.0e30
EPS_IN, EPS_ATTN = 1e-5, 1e-14
SRING = 3
LAG = 4
STEPS = 2 * CH


def build(nc, x, ctx_in, mask, wq, wk, wv, wo, w1, b1, w2, b2, gamma, beta,
          router_w, bias, gate_w, up_w, down_w, sh_gate, sh_up, sh_down, out):
    es = ExitStack()
    with es:
        es.enter_context(nc.allow_non_contiguous_dma(reason="two small vectors"))

        def sb(name, shape, dt=F32):
            return es.enter_context(nc.sbuf_tensor(name, shape, dt))

        def sem(name):
            return es.enter_context(nc.semaphore(name))

        x_all = sb("x_all", [P, NT, P])
        ctx_all = sb("ctx_all", [P, NT, P])
        mask_row = sb("mask_row", [P, T])
        mask_add = sb("mask_add", [P, CW])
        small_in = sb("small_in", [NE + NF, P])
        small_T = sb("small_T", [P, P])
        gam = sb("gam", [P, 2])
        bet = sb("bet", [P, 2])
        b2_row = sb("b2_row", [P, P])
        bias_row = sb("bias_row", [P, NE])
        wqk_in = sb("wqk_in", [P, 2, NH, P])
        wvo_in = sb("wvo_in", [P, 2, NH, P])
        wv_in, wo_in = wvo_in[:, 0], wvo_in[:, 1]
        w1_in = sb("w1_in", [P, NF * P])
        w2_in = sb("w2_in", [P, NF, P])
        w_exp = sb("w_exp", [P, NX, 3 * P])
        ident = sb("ident", [P, P])
        neg_half = sb("neg_half", [P, TPC])

        wT = sb("wT", [P, 3, NH, P])
        qk_hi, qk_lo = sb("qk_hi", [P, NH, P], F32R), sb("qk_lo", [P, NH, P], F32R)
        vo_hi, vo_lo = sb("vo_hi", [P, NH * P], F32R), sb("vo_lo", [P, NH * P], F32R)

        ctx_now = sb("ctx_now", [P, TPC, P])
        xnT_hi, xnT_lo = sb("xnT_hi", [P, CW], F32R), sb("xnT_lo", [P, CW], F32R)
        cT_hi, cT_lo = sb("cT_hi", [P, CW], F32R), sb("cT_lo", [P, CW], F32R)
        cT_m = sb("cT_m", [P, CW + SEQ])
        q_T = sb("q_T", [P, BPC, NH, SEQ])
        v_o = [sb(f"v_o{i}", [P, NH, P]) for i in range(2)]
        sc_m = [sb(f"sc_m{i}", [P, 2, HP, SEQ]) for i in range(SRING)]
        prob = [sb(f"prob{i}", [P, HP, 2, SEQ]) for i in range(2)]
        nmax = [sb(f"nmax{i}", [P, 2 * HP]) for i in range(SRING)]
        esum = [sb(f"esum{i}", [P, 2 * HP]) for i in range(SRING)]
        rsum = [sb(f"rsum{i}", [P, 2 * HP]) for i in range(SRING)]
        prob_T = [sb(f"prob_T{i}", [P, NH, 2, SEQ]) for i in range(2)]

        x1_b2 = sb("x1_b2", [P, TPC, P])
        x1_T = sb("x1_T", [P, CW])
        hid = sb("hid", [P, NF, CW])
        z = x1_b2
        xm_T = sb("xm_T", [P, CW])
        y = x2 = ctx_all
        x_beta = x_all
        mT_hi, mT_lo = sb("mT_hi", [P, T], F32R), sb("mT_lo", [P, T], F32R)
        logits = sb("logits", [P, NT, NE])

        cen = [sb(f"cen{i}", [P, TPC, P]) for i in range(4)]
        stat = [sb(f"stat{i}", [P, TPC, 6]) for i in range(4)]
        mean_var = [sb(f"mean_var{i}", [P, TPC, 2]) for i in range(4)]
        var_eps = [sb(f"var_eps{i}", [P, TPC]) for i in range(4)]
        rstd = [sb(f"rstd{i}", [P, TPC]) for i in range(4)]
        rstd_g = [sb(f"rstd_g{i}", [P, TPC]) for i in range(4)]
        xn, x1, ffn_n, xm = cen
        b2_beta = sb("b2_beta", [P, P])

        we_hi = [sb(f"we_hi{i}", [P, 3 * P], F32R) for i in range(2)]
        we_lo = [sb(f"we_lo{i}", [P, 3 * P], F32R) for i in range(2)]
        comb = [wqk_in[:].rearrange("p a h k -> p (a h k)"), wvo_in[:].rearrange("p a h k -> p (a h k)")]
        wT_flat = wT[:].rearrange("p a h k -> p (a h k)").rearrange("p (n t) -> p n t", t=CW)
        silu, s_u, act = ([wT_flat[:, 2 * a + i, :] for i in range(2)] for a in range(3))
        act_hi = [w[:].rearrange("p h k -> p (h k)")[:, i * CW:(i + 1) * CW] for w in (qk_hi, qk_lo) for i in range(2)]
        act_lo = [w[:, i * CW:(i + 1) * CW] for w in (vo_hi, vo_lo) for i in range(2)]
        comb_dram = nc.dram_tensor("comb_dram", [2, P, P], F32, kind="Internal").ap()

        r_e = q_T[:].rearrange("p b h s -> p (b h s)")

        def route_tile(n, width=NE):
            return r_e[:, n * NT * NE:n * NT * NE + NT * width].rearrange("p (t e) -> p t e", e=width)

        score, biased, picked, m_eq, m_gt, m_pre, m_pre2, m_tmp, comb_w = (route_tile(n) for n in range(9))
        pair_sum = r_e[:, 9 * NT * NE:9 * NT * NE + NT * NG * 6].rearrange("p (t g n) -> p t g n", g=NG, n=6)
        pool3 = sc_m[0][:].rearrange("p a b c -> p (a b c)")
        g_score = pool3[:, 0:NT * NG].rearrange("p (t g) -> p t g", g=NG)
        g_keep = pool3[:, NT * NG:2 * NT * NG].rearrange("p (t g) -> p t g", g=NG)
        g_rank = pool3[:, 2 * NT * NG:3 * NT * NG].rearrange("p (t g) -> p t g", g=NG)
        gg_a = sc_m[1][:].rearrange("p a b c -> p (a b c)")[:, 0:NT * 16].rearrange("p (t g k) -> p t g k", g=NG, k=NG)
        gg_b = sc_m[1][:].rearrange("p a b c -> p (a b c)")[:, NT * 16:].rearrange("p (t g k) -> p t g k", g=NG, k=NG)
        lower = sb("lower", [P, NG, NG])
        top8 = sb("top8", [P, NT, 8])
        n_gt = sb("n_gt", [P, NT])
        w_sum = sb("w_sum", [P, NT])
        w_inv = sb("w_inv", [P, NT])
        comb_T = sb("comb_T", [P, 2, P])

        bank = [es.enter_context(nc.psum_tensor(f"bank{i}", [P, CW], F32)) for i in range(8)]
        work = bank[0:3]
        sc_bank = bank[3:5]
        t_bank, av_bank, post_bank = bank[5], bank[6], bank[7]
        acc = [bank[0], bank[1], bank[2], bank[7]]
        h_bank, u_bank = [bank[3], bank[5]], [bank[4], bank[6]]

        ld_x0, ld_x, ld_c0, ld_c = sem("ld_x0"), sem("ld_x"), sem("ld_c0"), sem("ld_c")
        ld_mask, ld_small, ld_vec = sem("ld_mask"), sem("ld_small"), sem("ld_vec")
        ld_wq, ld_wk, ld_wv, ld_wo, ld_ffn = sem("ld_wq"), sem("ld_wk"), sem("ld_wv"), sem("ld_wo"), sem("ld_ffn")
        ld_exp = sem("ld_exp")
        const_step, ident_done, zero_done = sem("const_step"), sem("ident_done"), sem("zero_done")
        small_zero = sem("small_zero")
        small_turned, small_done = sem("small_turned"), sem("small_done")
        mask_done = sem("mask_done")
        w_turned = sem("w_turned")
        wT_done = [sem(f"wT_done{i}") for i in range(3)]
        fold_done = sem("fold_done")
        fold_hi, fold_lo = sem("fold_hi"), sem("fold_lo")
        stat_ready = [sem(f"stat_ready{i}") for i in range(4)]
        mean_var_ready = [sem(f"mean_var_ready{i}") for i in range(4)]
        var_ready = [sem(f"var_ready{i}") for i in range(4)]
        rstd_step = [sem(f"rstd_step{i}") for i in range(4)]
        rstd_ready = [sem(f"rstd_ready{i}") for i in range(4)]
        norm_ready = [sem(f"norm_ready{i}") for i in range(4)]
        ctx_now_ready, b2_beta_ready, x2_ready = sem("ctx_now_ready"), sem("b2_beta_ready"), sem("x2_ready")
        work_full = [sem(f"work_full{i}") for i in range(3)]
        work_free = [sem(f"work_free{i}") for i in range(3)]
        xnT_hi_ready, xnT_ready = sem("xnT_hi_ready"), sem("xnT_ready")
        cT_hi_ready, cT_lo_ready, cT_m_ready = sem("cT_hi_ready"), sem("cT_lo_ready"), sem("cT_m_ready")
        sc_full, sc_taken, max_ready = sem("sc_full"), sem("sc_taken"), sem("max_ready")
        sub_ready, exp_ready, sum_ready, rsum_ready = sem("sub_ready"), sem("exp_ready"), sem("sum_ready"), sem("rsum_ready")
        prob_ready, t_full, prob_T_ready = sem("prob_ready"), sem("t_full"), sem("prob_T_ready")
        av_full, y_ready = sem("av_full"), sem("y_ready")
        post_full, post_free = sem("post_full"), sem("post_free")
        x1_b2_ready, x_beta_ready = sem("x1_b2_ready"), sem("x_beta_ready")
        mT_hi_ready, xm_T_ready = sem("mT_hi_ready"), sem("xm_T_ready")
        exp_l_ready, route_step, route_done = sem("exp_l_ready"), sem("route_step"), sem("route_done")
        comb_turned, comb_T_ready, comb_stored = sem("comb_turned"), sem("comb_T_ready"), sem("comb_stored")
        ones_ready = sem("ones_ready")
        comb_loaded = [sem(f"comb_loaded{i}") for i in range(2)]
        gu_hi_ready, gu_lo_ready, dn_hi_ready, dn_lo_ready = sem("gu_hi_ready"), sem("gu_lo_ready"), sem("dn_hi_ready"), sem("dn_lo_ready")
        h_full, u_full, down_full = sem("h_full"), sem("u_full"), sem("down_full")
        silu_ready, s_u_ready, act_ready = sem("silu_ready"), sem("s_u_ready"), sem("act_ready")
        act_hi_ready, act_lo_ready = sem("act_hi_ready"), sem("act_lo_ready")
        acc_copied, out_turned, out_ready, stored = sem("acc_copied"), sem("out_turned"), sem("out_ready"), sem("stored")

        USES = 2 + NH + 2 * TPC
        per_slot = USES // 3
        assert USES % 3 == 0
        QUERY, VALUE = 2, 2 + NH

        def nth_use(c, k):
            return c * per_slot + (k // 3 + 1)

        def peeled(j):
            return isinstance(j, int) and j == 0

        FIRST = [(i, c) for i in range(2) for c in range(CH - 1)] + [(i, CH - 1) for i in range(2)]
        LATER = [(i, c) for i in range(2) for c in range(CH)]

        def slot_and_chunk(j, k):
            if k < 0:
                j, k = (j - 1 if isinstance(j, int) else 1), k + STEPS
            return (FIRST if peeled(j) else LATER)[k]

        POSTS = 6

        def post_count(c, k):
            return c * POSTS + k

        x_t = x.rearrange("b s d -> (b s) d").rearrange("(t p) d -> p t d", p=P)
        c_t = ctx_in.rearrange("b s d -> (b s) d").rearrange("(t p) d -> p t d", p=P)
        out_t = out.rearrange("b s d -> (b s) d").rearrange("(t p) d -> p t d", p=P)

        block = es.enter_context(nc.Block())

        @block.sync
        def _(sp):
            sp.dma_start(x_all[:, 0:TPC, :], x_t[:, 0:TPC, :]).then_inc(ld_x0, 16)
            sp.dma_start(ctx_all[:, 0:TPC, :], c_t[:, 0:TPC, :]).then_inc(ld_c0, 16)
            sp.dma_start(wv_in, wv.rearrange("h d v -> d h v")).then_inc(ld_wv, 16)
            sp.dma_start(wo_in, wo.rearrange("(h v) d -> v h d", v=P)).then_inc(ld_wo, 16)
            sp.dma_start(mask_row[:], mask.rearrange("b s -> (b s)").partition_broadcast(P)).then_inc(ld_mask, 16)
            sp.dma_start(x_all[:, TPC:, :], x_t[:, TPC:, :]).then_inc(ld_x, 16)
            sp.dma_start(ctx_all[:, TPC:, :], c_t[:, TPC:, :]).then_inc(ld_c, 16)
            sp.dma_start(w_exp[:, NSH:, 0:P], gate_w.rearrange("e d f -> d e f")).then_inc(ld_exp, 16)
            sp.dma_start(w_exp[:, NSH:, P:2 * P], up_w.rearrange("e d f -> d e f")).then_inc(ld_exp, 16)
            sp.dma_start(w_exp[:, NSH:, 2 * P:], down_w.rearrange("e f d -> f e d")).then_inc(ld_exp, 16)

            sp.wait_ge(comb_T_ready, 1)
            for half in range(2):
                sp.dma_start(comb_dram[half], comb_T[:, half, :]).then_inc(comb_stored, 16)
            sp.wait_ge(comb_stored, 32)
            by_expert = comb_dram.rearrange("a (t e) p -> e (a t) p", e=NE)

            def load_combine(j, i, used):
                sp.wait_ge(act_ready, used)
                sp.dma_start(comb[i].rearrange("p (a t) -> p a t", t=P),
                             by_expert[bass.ds(j * 2 + (i - NSH), 1)].rearrange("e a t -> (e a) t")
                             .partition_broadcast(P)).then_inc(comb_loaded[i], 16)

            load_combine(1, 0, STEPS - 1)
            load_combine(1, 1, STEPS)
            with sp.Fori(2, NX // 2) as j:
                load_combine(j, 0, j * STEPS - CH)
                load_combine(j, 1, j * STEPS)
            for c in range(CH):
                sp.wait_ge(out_ready, c + 1)
                sp.dma_start(out_t[:, c * TPC:(c + 1) * TPC, :],
                             x2[:, c * TPC:(c + 1) * TPC, :]).then_inc(stored, 16)
            sp.wait_ge(stored, 16 * CH)

        @block.gpsimd
        def _(pool):
            def inverse_root(n, c):
                pool.wait_ge(var_ready[n], c + 1)
                if n in (1, 2):
                    pool.tensor_tensor(rstd[n][:], var_eps[n][:], neg_half[:], ALU.pow).then_inc(rstd_step[n], 1)
                    pool.wait_ge(rstd_step[n], c + 1)
                    pool.tensor_scalar(rstd_g[n][:], rstd[n][:], gam[:, n - 1:n], None,
                                       ALU.mult).then_inc(rstd_ready[n], 1)
                else:
                    pool.tensor_tensor(rstd[n][:], var_eps[n][:], neg_half[:], ALU.pow).then_inc(rstd_ready[n], 1)

            def subtract_max(c, p):
                i = (c * TPC + p) % SRING
                pool.wait_ge(max_ready, c * TPC + (p + 1))
                pool.tensor_tensor(sc_m[i][:], sc_m[i][:],
                                   nmax[i][:].rearrange("p (b h) -> p b h", h=HP).unsqueeze(3)
                                   .to_broadcast([P, 2, HP, SEQ]), ALU.add).then_inc(sub_ready, 1)

            def normalise_probs(c, p):
                i = (c * TPC + p) % SRING
                pool.wait_ge(rsum_ready, c * TPC + (p + 1))
                if not (c == 0 and p < 2):
                    pool.wait_ge(t_full, c * TPC + (p - 1))
                pool.tensor_tensor(prob[p % 2][:].rearrange("p h b t -> p b h t"), sc_m[i][:],
                                   rsum[i][:].rearrange("p (b h) -> p b h", h=HP).unsqueeze(3)
                                   .to_broadcast([P, 2, HP, SEQ]), ALU.mult).then_inc(prob_ready, 1)

            def add_b2(c):
                pool.wait_ge(norm_ready[1], c + 1)
                pool.tensor_tensor(x1_b2[:], x1[:], b2_beta[:].unsqueeze(1).to_broadcast([P, TPC, P]),
                                   ALU.add).then_inc(x1_b2_ready, 1)

            def add_beta(c):
                pool.wait_ge(norm_ready[0], c + 1)
                now = x_all[:, c * TPC:(c + 1) * TPC, :]
                pool.tensor_scalar(now, now, bet[:, 1:2], None, ALU.add).then_inc(x_beta_ready, 1)

            pool.memset(ident[:], 1.0).then_inc(const_step, 1)
            pool.wait_ge(const_step, 1)
            pool.affine_select(out=ident[:], in_=ident[:], compare_op=ALU.is_equal, fill=0.0, base=0,
                               pattern=[[1, P]], channel_multiplier=-1).then_inc(ident_done, 1)
            pool.memset(neg_half[:], -0.5).then_inc(const_step, 1)
            pool.wait_ge(const_step, 2)
            inverse_root(0, 0)
            pool.memset(small_T[:], 0.0).then_inc(small_zero, 1)
            pool.memset(cT_m[:, CW:], 0.0)
            pool.memset(lower[:], 1.0).then_inc(const_step, 1)
            for i in range(2):
                z_last = pool.memset(prob_T[i][:], 0.0)
            z_last.then_inc(zero_done, 1)
            pool.wait_ge(const_step, 3)
            pool.affine_select(out=lower[:], in_=lower[:], compare_op=ALU.is_ge, fill=0.0, base=-1,
                               pattern=[[1, NG], [-1, NG]], channel_multiplier=0).then_inc(const_step, 1)
            pool.wait_ge(ld_vec, 64)
            pool.tensor_scalar(b2_beta[:], b2_row[:], bet[:, 0:1], None, ALU.add).then_inc(b2_beta_ready, 1)
            pool.wait_ge(b2_beta_ready, 1)

            for c in range(CH + 1):
                now, last, before = c < CH, c >= 1, c >= 2
                if last:
                    normalise_probs(c - 1, 3)
                if before:
                    inverse_root(2, c - 2)
                    inverse_root(3, c - 2)
                if last:
                    inverse_root(1, c - 1)
                if now:
                    subtract_max(c, 0)
                if last:
                    add_b2(c - 1)
                    add_beta(c - 1)
                if now:
                    subtract_max(c, 1)
                    normalise_probs(c, 0)
                    if c + 1 < CH:
                        inverse_root(0, c + 1)
                    subtract_max(c, 2)
                    normalise_probs(c, 1)
                    subtract_max(c, 3)
                    normalise_probs(c, 2)

            def split_lo(part, e, slot):
                a, b = (0, 2 * P) if part == "gu" else (2 * P, 3 * P)
                hi, lo = (gu_hi_ready, gu_lo_ready) if part == "gu" else (dn_hi_ready, dn_lo_ready)
                pool.wait_ge(hi, e + 1)
                pool.tensor_tensor(we_lo[slot][:, a:b], w_exp[:, bass.ds(e, 1), a:b].rearrange("p e n -> p (e n)"),
                                   we_hi[slot][:, a:b].bitcast(F32), ALU.subtract).then_inc(lo, 1)

            def weigh(j, k):
                i, c = slot_and_chunk(j, k)
                n = j * STEPS + k
                pool.wait_ge(s_u_ready, n + 1)
                if not peeled(j) and c == 0:
                    pool.wait_ge(comb_loaded[i], j * 16)
                if not (peeled(j) and k < 2):
                    pool.wait_ge(act_lo_ready, n - 1)
                pool.tensor_tensor(act[k % 2], s_u[k % 2], comb[i][:, c * CW:(c + 1) * CW],
                                   ALU.mult).then_inc(act_ready, 1)

            def experts(j, last):
                for k in range(STEPS):
                    if k == 0:
                        split_lo("gu", j * 2 + 1, 1)
                    if k == 3:
                        split_lo("dn", j * 2, 0)
                    if k == 4 and not last:
                        split_lo("gu", j * 2 + 2, 0)
                    if k == 5:
                        split_lo("dn", j * 2 + 1, 1)
                    weigh(j, k)

            pool.memset(comb[0], 1.0)
            pool.memset(comb[1], 1.0).then_inc(ones_ready, 1)
            pool.wait_ge(ones_ready, 1)
            for e in range(2):
                split_lo("gu", e, e)
                split_lo("dn", e, e)
            for k in range(5):
                weigh(0, k)
            inverse_root(2, CH - 1)
            weigh(0, 5)
            inverse_root(3, CH - 1)
            weigh(0, 6)
            split_lo("gu", 2, 0)
            weigh(0, 7)
            with pool.Fori(1, NX // 2 - 1) as j:
                experts(j, False)
            experts(NX // 2 - 1, True)

        @block.scalar
        def _(a):
            a.dma_start(wqk_in[:, 0], wq.rearrange("h d k -> d h k")).then_inc(ld_wq, 16)
            a.dma_start(wqk_in[:, 1], wk.rearrange("h d k -> d h k")).then_inc(ld_wk, 16)
            a.dma_start(small_in[0:NE, :], router_w).then_inc(ld_small, 16)
            a.dma_start(small_in[NE:NE + NF, :], b1.rearrange("(j f) -> j f", f=P)).then_inc(ld_small, 16)
            a.dma_start(gam[:], gamma.partition_broadcast(P)).then_inc(ld_vec, 16)
            a.dma_start(bet[:], beta.partition_broadcast(P)).then_inc(ld_vec, 16)
            a.dma_start(b2_row[:], b2.partition_broadcast(P)).then_inc(ld_vec, 16)
            a.dma_start(bias_row[:], bias.partition_broadcast(P)).then_inc(ld_vec, 16)
            a.dma_start(w1_in[:], w1).then_inc(ld_ffn, 16)
            a.dma_start(w2_in[:], w2.rearrange("(j f) d -> f j d", f=P)).then_inc(ld_ffn, 16)
            for i, w in enumerate((sh_gate, sh_up)):
                a.dma_start(w_exp[:, 0:NSH, i * P:(i + 1) * P], w.rearrange("d (e f) -> d e f", f=P)).then_inc(ld_exp, 16)
            a.dma_start(w_exp[:, 0:NSH, 2 * P:], sh_down.rearrange("(e f) d -> f e d", f=P)).then_inc(ld_exp, 16)

            def copy_ctx(c):
                if c:
                    a.wait_ge(work_full[1], nth_use(c - 1, 1))
                a.copy(ctx_now[:], ctx_all[:, bass.ts(c, TPC), :]).then_inc(ctx_now_ready, 1)

            def xnT_high(c):
                a.wait_ge(work_full[0], nth_use(c, 0))
                if c:
                    a.wait_ge(work_full[(VALUE - 1) % 3], nth_use(c - 1, VALUE - 1))
                a.copy(xnT_hi[:], work[0][:]).then_inc(xnT_hi_ready, 1)

            def cT_high(c):
                a.wait_ge(work_full[1], nth_use(c, 1))
                if c:
                    a.wait_ge(work_full[(USES - 1) % 3], nth_use(c - 1, USES - 1))
                a.copy(cT_hi[:], work[1][:]).then_inc(cT_hi_ready, 1)

            def query(c, h):
                k = QUERY + h
                a.wait_ge(work_full[k % 3], nth_use(c, k))
                if h == 0 and c:
                    a.wait_ge(sc_full, c * TPC)
                a.copy(q_T[:, :, h, :], work[k % 3][:].rearrange("p (b s) -> p b s", s=SEQ)
                       ).then_inc(work_free[k % 3], 1)

            def value(c, p):
                if not (c == 0 and p < 2):
                    a.wait_ge(av_full, c * TPC + (p - 1))
                for j in range(2):
                    k = VALUE + 2 * p + j
                    a.wait_ge(work_full[k % 3], nth_use(c, k))
                    a.copy(v_o[p % 2][:, j * HP:(j + 1) * HP, :].rearrange("p h d -> p (h d)"),
                           work[k % 3][:]).then_inc(work_free[k % 3], 1)

            def exponent(c, p):
                a.wait_ge(sub_ready, c * TPC + (p + 1))
                i = (c * TPC + p) % SRING
                a.activation(sc_m[i][:], sc_m[i][:], ACT.Exp).then_inc(exp_ready, 1)

            def spread(c, p):
                a.wait_ge(t_full, c * TPC + (p + 1))
                if not (c == 0 and p < 2):
                    a.wait_ge(av_full, c * TPC + (p - 1))
                for s in range(2):
                    rows = slice(s * SEQ, (s + 1) * SEQ)
                    last = a.copy(prob_T[p % 2][rows, :, s, :],
                                  t_bank[rows, :].rearrange("p (h s) -> p h s", s=SEQ))
                last.then_inc(prob_T_ready, 1)

            def turn_x1(c):
                a.wait_ge(post_full, c * POSTS + 1)
                a.activation(x1_T[:], post_bank[:], ACT.Identity, bias=bet[:, 0:1]).then_inc(post_free, 1)

            def hidden(c, j):
                a.wait_ge(post_full, c * POSTS + (2 + j))
                a.activation(hid[:, j, :], post_bank[:], ACT.Relu,
                             bias=small_T[:, NE + j:NE + j + 1]).then_inc(post_free, 1)

            def xm_high(c):
                a.wait_ge(post_full, c * POSTS + 5)
                a.copy(mT_hi[:, bass.ts(c, CW)], post_bank[:]).then_inc(mT_hi_ready, 1)
                a.copy(xm_T[:], post_bank[:]).then_inc(xm_T_ready, 1)

            a.wait_ge(ld_c0, 16)
            copy_ctx(0)
            for i in range(3):
                a.wait_ge(w_turned, 2 * i + 1)
                a.copy(wT[:, i, 0:HP, :].rearrange("p h d -> p (h d)"), bank[2 * i][:]).then_inc(wT_done[i], 1)
            a.wait_ge(small_turned, 1)
            a.wait_ge(small_zero, 1)
            a.copy(small_T[:, 0:NE + NF], bank[0][:, 0:NE + NF]).then_inc(small_done, 1)
            for i, (hi, half) in enumerate(((qk_hi, 0), (qk_hi, 1), (vo_hi, 0), (vo_hi, 1))):
                a.wait_ge(fold_done, i + 1)
                dst = hi[:, half * HP:(half + 1) * HP, :].rearrange("p h d -> p (h d)") if i < 2 else \
                    hi[:, half * CW:(half + 1) * CW]
                a.copy(dst, (bank[6], bank[7], bank[1], bank[2])[i][:]).then_inc(fold_hi, 1)
            a.wait_ge(small_done, 1)
            a.wait_ge(zero_done, 1)
            a.wait_ge(ld_vec, 64)

            for c in range(CH + 1):
                now, last, before = c < CH, c >= 1, c >= 2
                if last:
                    value(c - 1, 3)
                    spread(c - 1, 2)
                if now:
                    xnT_high(c)
                    cT_high(c)
                    query(c, 0)
                    query(c, 2)
                if last:
                    spread(c - 1, 3)
                if now:
                    query(c, 4)
                    query(c, 6)
                if before:
                    xm_high(c - 2)
                if not now:
                    break
                value(c, 0)
                exponent(c, 0)
                value(c, 1)
                if last:
                    turn_x1(c - 1)
                exponent(c, 1)
                spread(c, 0)
                value(c, 2)
                exponent(c, 2)
                if last:
                    hidden(c - 1, 0)
                spread(c, 1)
                if last:
                    hidden(c - 1, 1)
                if c + 1 < CH:
                    if c == 0:
                        a.wait_ge(ld_c, 16)
                    copy_ctx(c + 1)
                exponent(c, 3)

            def split_hi(part, e, slot):
                a0, b0 = (0, 2 * P) if part == "gu" else (2 * P, 3 * P)
                hi = gu_hi_ready if part == "gu" else dn_hi_ready
                a.copy(we_hi[slot][:, a0:b0],
                       w_exp[:, bass.ds(e, 1), a0:b0].rearrange("p e n -> p (e n)")).then_inc(hi, 1)

            def gate(j, k):
                n = j * STEPS + k
                a.wait_ge(h_full, n + 1)
                if not (peeled(j) and k < 2):
                    a.wait_ge(s_u_ready, n - 1)
                a.activation(silu[k % 2], h_bank[k % 2][:], ACT.Silu).then_inc(silu_ready, 1)

            def act_high(j, k):
                n = j * STEPS + k
                a.wait_ge(act_ready, n + 1)
                if not (peeled(j) and k < 4):
                    a.wait_ge(down_full, n - 3)
                a.copy(act_hi[k % 4], act[k % 2]).then_inc(act_hi_ready, 1)

            def experts(j, last):
                for k in range(STEPS):
                    if k == 0:
                        a.wait_ge(u_full, j * STEPS)
                        split_hi("gu", j * 2 + 1, 1)
                    if k == 3:
                        a.wait_ge(down_full, j * STEPS - 1)
                        split_hi("dn", j * 2, 0)
                    if k == 4 and not last:
                        a.wait_ge(u_full, j * STEPS + CH)
                        split_hi("gu", j * 2 + 2, 0)
                    if k == 5:
                        a.wait_ge(down_full, j * STEPS)
                        split_hi("dn", j * 2 + 1, 1)
                    gate(j, k)
                    act_high(j, k - 1)

            a.wait_ge(ld_exp, 6 * 16)
            for e in range(2):
                split_hi("gu", e, e)
                split_hi("dn", e, e)
            gate(0, 0)
            turn_x1(CH - 1)
            gate(0, 1)
            act_high(0, 0)
            hidden(CH - 1, 0)
            gate(0, 2)
            act_high(0, 1)
            hidden(CH - 1, 1)
            for k in range(3, 6):
                gate(0, k)
                act_high(0, k - 1)
            act_high(0, 5)
            xm_high(CH - 1)
            a.wait_ge(post_free, POSTS * CH)
            a.activation(score, logits[:], ACT.Exp, scale=-1.0).then_inc(exp_l_ready, 1)
            gate(0, 6)
            gate(0, 7)
            act_high(0, 6)
            a.wait_ge(u_full, STEPS - 1)
            split_hi("gu", 2, 0)
            with a.Fori(1, NX // 2 - 1) as j:
                experts(j, False)
            experts(NX // 2 - 1, True)
            act_high(NX // 2, -1)
            for c in range(0, CH, 2):
                a.wait_ge(down_full, NX * CH - CH + c + 1)
                a.copy(q_T[:, 2 * c:2 * c + 2].rearrange("p b h s -> p (b h s)")[:, 0:CW], acc[c][:]).then_inc(acc_copied, 1)

        @block.vector
        def _(v):
            def statistics(n, c, src):
                for t in range(TPC):
                    last = v.bn_stats(stat[n][:, t, :], src[:, t, :])
                last.then_inc(stat_ready[n], 1)
                v.wait_ge(stat_ready[n], c + 1)
                for t in range(TPC):
                    last = v.bn_aggr(mean_var[n][:, t, :], stat[n][:, t, :])
                last.then_inc(mean_var_ready[n], 1)
                v.wait_ge(mean_var_ready[n], c + 1)
                v.tensor_scalar(var_eps[n][:], mean_var[n][:, :, 1], EPS_ATTN if n in (1, 2) else EPS_IN, None,
                                ALU.add).then_inc(var_ready[n], 1)

            def normalise(n, c, src):
                v.wait_ge(rstd_ready[n], c + 1)
                by = rstd_g if n in (1, 2) else rstd
                for t in range(TPC):
                    last = v.tensor_scalar(cen[n][:, t, :], src[:, t, :], mean_var[n][:, t, 0:1], by[n][:, t:t + 1],
                                           ALU.subtract, ALU.mult)
                last.then_inc(norm_ready[n], 1)

            def tokens(t, c):
                return t[:, c * TPC:(c + 1) * TPC, :]

            def residual(c):
                normalise(2, c, z)
                v.wait_ge(norm_ready[2], c + 1)
                v.wait_ge(x_beta_ready, c + 1)
                v.tensor_tensor(tokens(x2, c), ffn_n[:], tokens(x_beta, c), ALU.add).then_inc(x2_ready, 1)
                v.wait_ge(x2_ready, c + 1)

            def xnT_low(c):
                v.wait_ge(xnT_hi_ready, c + 1)
                v.tensor_tensor(xnT_lo[:], work[0][:], xnT_hi[:].bitcast(F32), ALU.subtract).then_inc(work_free[0], 1)

            def cT_low(c):
                v.wait_ge(cT_hi_ready, c + 1)
                v.tensor_tensor(cT_lo[:], work[1][:], cT_hi[:].bitcast(F32), ALU.subtract).then_inc(cT_lo_ready, 1)
                if c:
                    v.wait_ge(sc_full, c * TPC)
                v.tensor_tensor(cT_m[:, 0:CW], work[1][:], mask_row[:, bass.ts(c, CW)],
                                ALU.mult).then_inc(work_free[1], 1)
                v.tensor_scalar(mask_add[:], mask_row[:, bass.ts(c, CW)], -1.0, BIG, ALU.add,
                                ALU.mult).then_inc(mask_done, 1)

            def query(c, h):
                k = QUERY + h
                v.wait_ge(work_full[k % 3], nth_use(c, k))
                v.tensor_copy(q_T[:, :, h, :], work[k % 3][:].rearrange("p (b s) -> p b s", s=SEQ)
                              ).then_inc(work_free[k % 3], 1)

            def mask_and_max(c, p):
                i = (c * TPC + p) % SRING
                if c * TPC + p >= SRING:
                    v.wait_ge(prob_ready, c * TPC + p - SRING + 1)
                v.wait_ge(sc_full, c * TPC + (p + 1))
                v.wait_ge(mask_done, c + 1)
                for s in range(2):
                    last = v.tensor_tensor(
                        sc_m[i][:, s], sc_bank[s][:].rearrange("p (h t) -> p h t", t=P)[:, :, 0:SEQ],
                        mask_add[:, (2 * p + s) * SEQ:(2 * p + s + 1) * SEQ].unsqueeze(1)
                        .to_broadcast([P, HP, SEQ]), ALU.add)
                last.then_inc(sc_taken, 1)
                v.wait_ge(sc_taken, c * TPC + (p + 1))
                v.tensor_reduce(nmax[i][:].rearrange("p (b h) -> p b h", h=HP), sc_m[i][:], AX.X, ALU.max,
                                negate=True).then_inc(max_ready, 1)

            def sum_of_exp(c, p):
                i = (c * TPC + p) % SRING
                v.wait_ge(exp_ready, c * TPC + (p + 1))
                v.tensor_reduce(esum[i][:].rearrange("p (b h) -> p b h", h=HP), sc_m[i][:], AX.X,
                                ALU.add).then_inc(sum_ready, 1)
                v.wait_ge(sum_ready, c * TPC + (p + 1))
                v.reciprocal(rsum[i][:], esum[i][:]).then_inc(rsum_ready, 1)

            def add_ctx(c, p):
                v.wait_ge(av_full, c * TPC + (p + 1))
                tile = y[:, bass.ds(c * TPC + p, 1), :].rearrange("p o d -> p (o d)")
                v.tensor_tensor(tile, av_bank[:, 0:P], tile, ALU.add).then_inc(y_ready, 1)

            def add_ffn(c):
                v.wait_ge(post_full, c * POSTS + 4)
                v.wait_ge(x1_b2_ready, c + 1)
                v.tensor_tensor(z[:], post_bank[:].rearrange("p (t d) -> p t d", d=P), x1_b2[:],
                                ALU.add).then_inc(post_free, 1)
                v.wait_ge(post_free, c * POSTS + 4)

            def xm_low(c):
                v.wait_ge(mT_hi_ready, c + 1)
                v.wait_ge(xm_T_ready, c + 1)
                v.tensor_tensor(mT_lo[:, bass.ts(c, CW)], post_bank[:], mT_hi[:, bass.ts(c, CW)].bitcast(F32),
                                ALU.subtract).then_inc(post_free, 1)
                v.wait_ge(post_full, c * POSTS + 6)
                v.tensor_copy(logits[:, bass.ts(c, TPC), :],
                              post_bank[:].rearrange("p (t n) -> p t n", n=P)[:, :, 0:NE]).then_inc(post_free, 1)

            v.wait_ge(ld_x0, 16)
            statistics(0, 0, tokens(x_all, 0))
            for i in range(2):
                v.wait_ge(w_turned, 2 * i + 2)
                v.tensor_copy(wT[:, i, HP:, :].rearrange("p h d -> p (h d)"), bank[2 * i + 1][:]).then_inc(wT_done[i], 1)
            v.wait_ge(w_turned, 6)
            v.tensor_copy(wT[:, 2, HP:, :].rearrange("p h d -> p (h d)"), bank[5][:]).then_inc(wT_done[2], 1)
            normalise(0, 0, tokens(x_all, 0))
            for i, (hi, lo, half) in enumerate(((qk_hi, qk_lo, 0), (qk_hi, qk_lo, 1), (vo_hi, vo_lo, 0), (vo_hi, vo_lo, 1))):
                v.wait_ge(fold_hi, i + 1)
                dst, src = (w[:, half * HP:(half + 1) * HP, :].rearrange("p h d -> p (h d)") if i < 2 else
                            w[:, half * CW:(half + 1) * CW] for w in (lo, hi))
                v.tensor_tensor(dst, (bank[6], bank[7], bank[1], bank[2])[i][:], src.bitcast(F32),
                                ALU.subtract).then_inc(fold_lo, 1)
            v.wait_ge(ld_mask, 16)
            v.wait_ge(ld_c0, 16)

            for c in range(CH + 1):
                now, last, before = c < CH, c >= 1, c >= 2
                if before:
                    add_ffn(c - 2)
                if last:
                    sum_of_exp(c - 1, 3)
                if before:
                    statistics(2, c - 2, z)
                if now:
                    xnT_low(c)
                    cT_low(c)
                if last:
                    add_ctx(c - 1, 2)
                if now:
                    query(c, 1)
                if before:
                    residual(c - 2)
                if now:
                    query(c, 3)
                if before:
                    statistics(3, c - 2, tokens(x2, c - 2))
                if now:
                    query(c, 5)
                    query(c, 7)
                if before:
                    normalise(3, c - 2, tokens(x2, c - 2))
                if last:
                    add_ctx(c - 1, 3)
                    v.wait_ge(y_ready, c * TPC)
                    statistics(1, c - 1, tokens(y, c - 1))
                if before:
                    xm_low(c - 2)
                if now:
                    mask_and_max(c, 0)
                if last:
                    normalise(1, c - 1, tokens(y, c - 1))
                if not now:
                    break
                mask_and_max(c, 1)
                if c + 1 < CH:
                    if c == 0:
                        v.wait_ge(ld_x, 16)
                        v.wait_ge(ld_c, 16)
                    statistics(0, c + 1, tokens(x_all, c + 1))
                sum_of_exp(c, 0)
                mask_and_max(c, 2)
                sum_of_exp(c, 1)
                if c + 1 < CH:
                    normalise(0, c + 1, tokens(x_all, c + 1))
                add_ctx(c, 0)
                mask_and_max(c, 3)
                sum_of_exp(c, 2)
                add_ctx(c, 1)

            steps = [0]

            def done(ins):
                steps[0] += 1
                ins.then_inc(route_step, 1)
                v.wait_ge(route_step, steps[0])

            def by_token(t, n):
                return t[:].unsqueeze(2).to_broadcast([P, NT, n])

            def sigmoid_and_groups():
                v.wait_ge(exp_l_ready, 1)
                v.wait_ge(const_step, 4)
                done(v.tensor_scalar(m_tmp, score, 1.0, None, ALU.add))
                done(v.reciprocal(score, m_tmp))
                done(v.tensor_tensor(biased, score, bias_row[:].unsqueeze(1).to_broadcast([P, NT, NE]), ALU.add))
                s4 = biased.rearrange("p t (g n) -> p t g n", n=EPG)
                v.tensor_tensor(pair_sum[:, :, :, 0:3], s4[:, :, :, 0:3], s4[:, :, :, 1:4], ALU.add)
                v.tensor_tensor(pair_sum[:, :, :, 3:5], s4[:, :, :, 0:2], s4[:, :, :, 2:4], ALU.add)
                done(v.tensor_tensor(pair_sum[:, :, :, 5:6], s4[:, :, :, 0:1], s4[:, :, :, 3:4], ALU.add))
                done(v.tensor_reduce(g_score, pair_sum, AX.X, ALU.max))

            def keep_groups():
                mine = g_score.unsqueeze(3).to_broadcast([P, NT, NG, NG])
                other = g_score.unsqueeze(2).to_broadcast([P, NT, NG, NG])
                before = lower[:].unsqueeze(1).to_broadcast([P, NT, NG, NG])
                done(v.tensor_tensor(gg_a, other, mine, ALU.is_equal))
                done(v.tensor_tensor(gg_b, gg_a, before, ALU.mult))
                done(v.tensor_tensor(gg_a, other, mine, ALU.is_gt))
                done(v.tensor_tensor(gg_a, gg_a, gg_b, ALU.add))
                done(v.tensor_reduce(g_rank, gg_a, AX.X, ALU.add))
                done(v.tensor_scalar(g_keep, g_rank, 1.5, None, ALU.is_lt))
                done(v.tensor_scalar(g_rank, g_keep, -1.0, None, ALU.add))
                keep = g_keep.unsqueeze(3).to_broadcast([P, NT, NG, EPG])
                less = g_rank.unsqueeze(3).to_broadcast([P, NT, NG, EPG])
                done(v.tensor_tensor(m_tmp.rearrange("p t (g n) -> p t g n", n=EPG),
                                     biased.rearrange("p t (g n) -> p t g n", n=EPG), keep, ALU.mult))
                done(v.tensor_tensor(picked.rearrange("p t (g n) -> p t g n", n=EPG),
                                     m_tmp.rearrange("p t (g n) -> p t g n", n=EPG), less, ALU.add))

            def keep_experts():
                for t in range(NT):
                    last = v.max(top8[:, t, :], picked[:, t, :])
                done(last)
                fourth = top8[:, :, TOPK - 1:TOPK].to_broadcast([P, NT, NE])
                done(v.tensor_tensor(m_gt, picked, fourth, ALU.is_gt))
                done(v.tensor_tensor(m_eq, picked, fourth, ALU.is_equal))
                done(v.tensor_reduce(n_gt[:], m_gt, AX.X, ALU.add))
                src, dst = m_eq, m_pre
                for step in (1, 2, 4, 8):
                    v.tensor_copy(dst[:, :, 0:step], src[:, :, 0:step])
                    done(v.tensor_tensor(dst[:, :, step:], src[:, :, step:], src[:, :, 0:NE - step], ALU.add))
                    src, dst = dst, (m_pre2 if dst is m_pre else m_pre)
                done(v.tensor_tensor(m_tmp, src, by_token(n_gt, NE), ALU.add))
                done(v.tensor_scalar(m_tmp, m_tmp, TOPK + 0.5, None, ALU.is_lt))
                done(v.tensor_tensor(m_tmp, m_tmp, m_eq, ALU.mult))
                done(v.tensor_tensor(m_tmp, m_tmp, m_gt, ALU.add))

            def combine():
                done(v.tensor_tensor(m_gt, m_tmp, score, ALU.mult))
                done(v.tensor_reduce(w_sum[:], m_gt, AX.X, ALU.add))
                done(v.tensor_scalar(w_sum[:], w_sum[:], 1e-20, None, ALU.add))
                done(v.reciprocal(w_inv[:], w_sum[:]))
                done(v.tensor_tensor(m_tmp, m_gt, by_token(w_inv, NE), ALU.mult))
                v.tensor_scalar(comb_w, m_tmp, ROUTE_SCALE, None, ALU.mult).then_inc(route_done, 1)

            def gate_up(j, k):
                n = j * STEPS + k
                v.wait_ge(silu_ready, n + 1)
                v.wait_ge(u_full, n + 1)
                if not (peeled(j) and k < 2):
                    v.wait_ge(act_ready, n - 1)
                v.tensor_tensor(s_u[k % 2], u_bank[k % 2][:], silu[k % 2], ALU.mult).then_inc(s_u_ready, 1)

            def act_low(j, k):
                n = j * STEPS + k
                v.wait_ge(act_hi_ready, n + 1)
                v.tensor_tensor(act_lo[k % 4], act[k % 2], act_hi[k % 4].bitcast(F32),
                                ALU.subtract).then_inc(act_lo_ready, 1)

            gate_up(0, 0)
            gate_up(0, 1)
            act_low(0, 0)
            gate_up(0, 2)
            act_low(0, 1)
            gate_up(0, 3)
            act_low(0, 2)
            add_ffn(CH - 1)
            statistics(2, CH - 1, z)
            gate_up(0, 4)
            act_low(0, 3)
            residual(CH - 1)
            statistics(3, CH - 1, tokens(x2, CH - 1))
            gate_up(0, 5)
            act_low(0, 4)
            normalise(3, CH - 1, tokens(x2, CH - 1))
            act_low(0, 5)
            xm_low(CH - 1)
            sigmoid_and_groups()
            keep_groups()
            gate_up(0, 6)
            gate_up(0, 7)
            act_low(0, 6)
            keep_experts()
            combine()
            v.wait_ge(comb_turned, 1)
            v.tensor_copy(comb_T[:], post_bank[:, 0:2 * P].rearrange("p (a t) -> p a t", t=P)).then_inc(comb_T_ready, 1)
            with v.Fori(1, NX // 2) as j:
                for k in range(STEPS):
                    gate_up(j, k)
                    act_low(j, k - 1)
            act_low(NX // 2, -1)
            for c in range(1, CH, 2):
                v.wait_ge(down_full, NX * CH - CH + c + 1)
                v.tensor_copy(q_T[:, 2 * c:2 * c + 2].rearrange("p b h s -> p (b h s)")[:, 0:CW], acc[c][:]).then_inc(acc_copied, 1)
            for c in range(CH):
                v.wait_ge(out_turned, c + 1)
                v.tensor_tensor(x2[:, c * TPC:(c + 1) * TPC, :], (h_bank + u_bank)[c][:].rearrange("p (t d) -> p t d", d=P),
                                x2[:, c * TPC:(c + 1) * TPC, :], ALU.add).then_inc(out_ready, 1)

        @block.tensor
        def _(pe):
            def three(dst, w_hi, w_lo, m_hi, m_lo, start, stop):
                pe.matmul(dst, w_hi, m_hi, start=start, stop=False)
                pe.matmul(dst, w_hi, m_lo, start=False, stop=False)
                return pe.matmul(dst, w_lo, m_hi, start=False, stop=stop)

            def work_bank(c, k):
                if not (c == 0 and k < 3):
                    pe.wait_ge(work_free[k % 3], nth_use(c, k) - 1)
                return work[k % 3]

            def turn_inputs(c):
                w = work_bank(c, 0)
                pe.wait_ge(norm_ready[0], c + 1)
                for t in range(TPC):
                    last = pe.transpose(w[:, t * P:(t + 1) * P], xn[:, t, :], ident[:])
                last.then_inc(work_full[0], 1)
                w = work_bank(c, 1)
                pe.wait_ge(ctx_now_ready, c + 1)
                for t in range(TPC):
                    last = pe.transpose(w[:, t * P:(t + 1) * P], ctx_now[:, t, :], ident[:])
                last.then_inc(work_full[1], 1)

            def queries(c, heads):
                pe.wait_ge(work_free[0], nth_use(c, 0))
                for h in heads:
                    k = QUERY + h
                    w = work_bank(c, k)
                    three(w[:], qk_hi[:, h, :], qk_lo[:, h, :], xnT_hi[:], xnT_lo[:], True, True
                          ).then_inc(work_full[k % 3], 1)

            def values(c, p):
                if p == 0:
                    pe.wait_ge(cT_lo_ready, c + 1)
                tok = slice(p * P, (p + 1) * P)
                for j in range(2):
                    k = VALUE + 2 * p + j
                    w = work_bank(c, k)
                    cols = slice(j * CW, (j + 1) * CW)
                    three_moving(w[:], cT_hi[:, tok], cT_lo[:, tok], vo_hi[:, cols], vo_lo[:, cols]
                                 ).then_inc(work_full[k % 3], 1)

            def three_moving(dst, w_hi, w_lo, m_hi, m_lo):
                return three(dst, w_hi, w_lo, m_hi, m_lo, True, True)

            def scores(c, p):
                if p == 0:
                    for k in range(VALUE - 3, VALUE):
                        pe.wait_ge(work_free[k % 3], nth_use(c, k))
                    pe.wait_ge(work_free[1], nth_use(c, 1))
                if not (c == 0 and p == 0):
                    pe.wait_ge(sc_taken, c * TPC + p)
                for s in range(2):
                    b = 2 * p + s
                    for hp in range(HP):
                        last = pe.matmul(sc_bank[s][:, hp * P:(hp + 1) * P],
                                         q_T[:, b, 2 * hp:2 * hp + 2, :].rearrange("p h s -> p (h s)"),
                                         cT_m[:, b * SEQ:b * SEQ + P], start=True, stop=True)
                last.then_inc(sc_full, 1)

            def turn_probs(c, p):
                pe.wait_ge(prob_ready, c * TPC + (p + 1))
                if not (c == 0 and p == 0):
                    pe.wait_ge(prob_T_ready, c * TPC + p)
                for hp in range(HP):
                    last = pe.transpose(t_bank[:, hp * P:(hp + 1) * P],
                                        prob[p % 2][:, hp, :, :].rearrange("p b t -> p (b t)"), ident[:])
                last.then_inc(t_full, 1)

            def attend(c, p):
                pe.wait_ge(prob_T_ready, c * TPC + (p + 1))
                for j in range(2):
                    k = VALUE + 2 * p + j
                    pe.wait_ge(work_free[k % 3], nth_use(c, k))
                if not (c == 0 and p == 0):
                    pe.wait_ge(y_ready, c * TPC + p)
                for h in range(NH):
                    last = pe.matmul(av_bank[:, 0:P], prob_T[p % 2][:, h, :, :].rearrange("p b s -> p (b s)"),
                                     v_o[p % 2][:, h, :], start=(h == 0), stop=(h == NH - 1))
                last.then_inc(av_full, 1)

            def post_bank_for(c, k):
                pe.wait_ge(post_free, post_count(c, k))

            def turn_x1(c):
                pe.wait_ge(norm_ready[1], c + 1)
                if c:
                    pe.wait_ge(post_free, post_count(c, 0))
                for t in range(TPC):
                    last = pe.transpose(post_bank[:, t * P:(t + 1) * P], x1[:, t, :], ident[:])
                last.then_inc(post_full, 1)

            def ffn_up(c, j):
                post_bank_for(c, 1 + j)
                pe.matmul(post_bank[:], w1_in[:, j * P:(j + 1) * P], x1_T[:],
                          start=True, stop=True).then_inc(post_full, 1)

            def ffn_down(c):
                post_bank_for(c, 3)
                for t in range(TPC):
                    for j in range(NF):
                        last = pe.matmul(post_bank[:, t * P:(t + 1) * P], hid[:, j, t * P:(t + 1) * P],
                                         w2_in[:, j, :], start=(j == 0), stop=(j == NF - 1))
                last.then_inc(post_full, 1)

            def turn_xm(c):
                post_bank_for(c, 4)
                pe.wait_ge(norm_ready[3], c + 1)
                for t in range(TPC):
                    last = pe.transpose(post_bank[:, t * P:(t + 1) * P], xm[:, t, :], ident[:])
                last.then_inc(post_full, 1)

            def route(c):
                post_bank_for(c, 5)
                pe.wait_ge(xm_T_ready, c + 1)
                for t in range(TPC):
                    last = pe.matmul(post_bank[:, t * P:(t + 1) * P], xm_T[:, t * P:(t + 1) * P], small_T[:],
                                     start=True, stop=True)
                last.then_inc(post_full, 1)

            pe.wait_ge(ident_done, 1)
            for i, ready in enumerate((ld_wq, ld_wk, ld_wv)):
                pe.wait_ge(ready, 16)
                for half in range(2):
                    for h in range(HP):
                        src = wqk_in[:, i, half * HP + h, :] if i < 2 else wv_in[:, half * HP + h, :]
                        last = pe.transpose(bank[2 * i + half][:, h * P:(h + 1) * P], src, ident[:])
                    last.then_inc(w_turned, 1)
            for i in range(2):
                pe.wait_ge(wT_done[i], 2)
            for half in range(2):
                for h in range(HP):
                    hh = half * HP + h
                    last = pe.matmul(bank[6 + half][:, h * P:(h + 1) * P], wT[:, 0, hh, :], wT[:, 1, hh, :],
                                     start=True, stop=True)
                last.then_inc(fold_done, 1)
            pe.wait_ge(ld_small, 32)
            pe.transpose(bank[0][:, 0:NE + NF], small_in[:], ident[0:NE + NF, 0:NE + NF]).then_inc(small_turned, 1)
            pe.wait_ge(wT_done[2], 2)
            pe.wait_ge(ld_wo, 16)
            for half in range(2):
                for h in range(HP):
                    hh = half * HP + h
                    last = pe.matmul(bank[1 + half][:, h * P:(h + 1) * P], wT[:, 2, hh, :], wo_in[:, hh, :],
                                     start=True, stop=True)
                last.then_inc(fold_done, 1)
            pe.wait_ge(small_done, 1)
            pe.wait_ge(fold_lo, 4)
            pe.wait_ge(zero_done, 1)
            pe.wait_ge(ld_ffn, 32)

            for c in range(CH + 1):
                now, last, before = c < CH, c >= 1, c >= 2
                if last:
                    values(c - 1, 3)
                    turn_probs(c - 1, 2)
                if now:
                    turn_inputs(c)
                if last:
                    attend(c - 1, 2)
                if now:
                    queries(c, range(0, 4))
                if last:
                    turn_probs(c - 1, 3)
                if now:
                    queries(c, range(4, NH))
                if last:
                    attend(c - 1, 3)
                if before:
                    turn_xm(c - 2)
                    route(c - 2)
                if not now:
                    break
                scores(c, 0)
                values(c, 0)
                scores(c, 1)
                values(c, 1)
                if last:
                    turn_x1(c - 1)
                scores(c, 2)
                turn_probs(c, 0)
                values(c, 2)
                attend(c, 0)
                if last:
                    ffn_up(c - 1, 0)
                turn_probs(c, 1)
                if last:
                    ffn_up(c - 1, 1)
                scores(c, 3)
                attend(c, 1)
                if last:
                    ffn_down(c - 1)

            def turn_combine():
                pe.wait_ge(route_done, 1)
                for half in range(2):
                    last = pe.transpose(post_bank[:, half * P:(half + 1) * P],
                                        comb_w.rearrange("p t e -> p (t e)")[:, half * P:(half + 1) * P], ident[:])
                last.then_inc(comb_turned, 1)
                pe.wait_ge(comb_T_ready, 1)

            def up(j, k):
                n = j * STEPS + k
                i, c = slot_and_chunk(j, k)
                if c == 0:
                    pe.wait_ge(gu_lo_ready, j * 2 + (i + 1))
                cols = slice(c * CW, (c + 1) * CW)
                if not (peeled(j) and k < 2):
                    pe.wait_ge(silu_ready, n - 1)
                three(h_bank[k % 2][:], we_hi[i][:, 0:P], we_lo[i][:, 0:P], mT_hi[:, cols], mT_lo[:, cols],
                      True, True).then_inc(h_full, 1)
                if not (peeled(j) and k < 2):
                    pe.wait_ge(s_u_ready, n - 1)
                three(u_bank[k % 2][:], we_hi[i][:, P:2 * P], we_lo[i][:, P:2 * P], mT_hi[:, cols], mT_lo[:, cols],
                      True, True).then_inc(u_full, 1)

            def down(j, k, start=False, stop=False):
                n = j * STEPS + k
                i, c = slot_and_chunk(j, k)
                if c == 0:
                    pe.wait_ge(dn_lo_ready, j * 2 + (i + 1) - (2 if k < 0 else 0))
                pe.wait_ge(act_lo_ready, n + 1)
                three(acc[c][:], we_hi[i][:, 2 * P:], we_lo[i][:, 2 * P:], act_hi[k % 4], act_lo[k % 4],
                      start, stop).then_inc(down_full, 1)

            for k in range(6):
                up(0, k)
                if k == 0:
                    turn_x1(CH - 1)
                if k == 1:
                    ffn_up(CH - 1, 0)
                if k == 2:
                    ffn_up(CH - 1, 1)
                if k == 3:
                    ffn_down(CH - 1)
                if k >= LAG:
                    down(0, k - LAG, start=True)
            turn_xm(CH - 1)
            route(CH - 1)
            up(0, 6)
            down(0, 2, start=True)
            up(0, 7)
            down(0, 3)
            turn_combine()
            for k in range(STEPS):
                up(1, k)
                down(1, k - LAG, start=(k - LAG == FIRST.index((0, CH - 1)) - STEPS))
            with pe.Fori(2, NX // 2) as j:
                for k in range(STEPS):
                    up(j, k)
                    down(j, k - LAG)
            for k in range(-LAG, 0):
                down(NX // 2, k, stop=True)
            for c in range(CH):
                pe.wait_ge(acc_copied, CH)
                dst = (h_bank + u_bank)[c]
                src = q_T[:, 2 * c:2 * c + 2].rearrange("p b h s -> p (b h s)")
                for t in range(TPC):
                    last = pe.transpose(dst[:, t * P:(t + 1) * P], src[:, t * P:(t + 1) * P], ident[:])
                last.then_inc(out_turned, 1)


_INS = ['x', 'ctx_1024', 'mask_BxS2_ff1', 'L0_xattn_Wq', 'L0_xattn_Wk', 'L0_xattn_Wv', 'L0_xattn_Wo', 'L0_xattn_W1',
        'L0_xattn_b1', 'L0_xattn_W2', 'L0_xattn_b2', 'L0_xattn_gamma', 'L0_xattn_beta', 'L0_ffn_router_w',
        'L0_ffn_bias', 'L0_ffn_gate_w', 'L0_ffn_up_w', 'L0_ffn_down_w', 'L0_ffn_sh_gate_w', 'L0_ffn_sh_up_w',
        'L0_ffn_sh_down_w']


def kernel(**inputs):
    import concourse.bacc as bacc
    from concourse.bass_utils import run_bass_kernel_spmd

    nc = bacc.Bacc("TRN2", target_bir_lowering=False, num_devices=1)
    arrays, args = {}, []
    for name in _INS:
        a = np.ascontiguousarray(inputs[name])
        arrays[f"in_{name}"] = a
        args.append(nc.dram_tensor(f"in_{name}", a.shape, mybir.dt.from_np(a.dtype), kind="ExternalInput").ap())
    args.append(nc.dram_tensor("out_x", (NB, SEQ, P), F32, kind="ExternalOutput").ap())
    build(nc, *args)
    r = run_bass_kernel_spmd(nc, [arrays], core_ids=[0])
    return r.results[0]["out_x"]
```

```python
from contextlib import ExitStack

import concourse.bass as bass
import concourse.mybir as mybir
import numpy as np

F32 = mybir.dt.float32
F32R = mybir.dt.float32r
ALU = mybir.AluOpType
ACT = mybir.ActivationFunctionType
AX = mybir.AxisListType

P = 128
NB, SEQ = 32, 64
T = NB * SEQ
NT = T // P
CH = 4
TPC = NT // CH
CW = T // CH
BPC = NB // CH
NH = 8
HP = NH // 2
NF = 2
NSH = 2
NE = 16
NX = NSH + NE
NG, EPG = 4, 4
TOPK = 4
MARK, TAKEN = 3.0e38, -3.0e38
ROUTE_SCALE = 2.5
BIG = 1.0e30
EPS_IN, EPS_ATTN = 1e-5, 1e-14
SRING = 3
LAG = 4
STEPS = 2 * CH
FEW = 2 * STEPS


def build(nc, x, ctx_in, mask, wq, wk, wv, wo, w1, b1, w2, b2, gamma, beta,
          router_w, bias, gate_w, up_w, down_w, sh_gate, sh_up, sh_down, out):
    es = ExitStack()
    with es:
        es.enter_context(nc.allow_non_contiguous_dma(reason="two small vectors"))

        def sb(name, shape, dt=F32):
            return es.enter_context(nc.sbuf_tensor(name, shape, dt))

        def sem(name):
            return es.enter_context(nc.semaphore(name))

        x_all = sb("x_all", [P, NT, P])
        ctx_all = sb("ctx_all", [P, NT, P])
        mask_row = sb("mask_row", [P, T])
        mask_add = sb("mask_add", [P, CW])
        small_in = sb("small_in", [NE + NF, P])
        small_T = sb("small_T", [P, P])
        gam = sb("gam", [P, 2])
        bet = sb("bet", [P, 2])
        b2_row = sb("b2_row", [P, P])
        bias_row = sb("bias_row", [P, NE])
        wqk_in = sb("wqk_in", [P, 2, NH, P])
        wvo_in = sb("wvo_in", [P, 2, NH, P])
        wv_in, wo_in = wvo_in[:, 0], wvo_in[:, 1]
        w1_in = sb("w1_in", [P, NF * P])
        w2_in = sb("w2_in", [P, NF, P])
        w_exp = sb("w_exp", [P, NX, 3 * P])
        ident = sb("ident", [P, P])
        neg_half = sb("neg_half", [P, TPC])

        wT = sb("wT", [P, 3, NH, P])
        qk_hi, qk_lo = sb("qk_hi", [P, NH, P], F32R), sb("qk_lo", [P, NH, P], F32R)
        vo_hi, vo_lo = sb("vo_hi", [P, NH * P], F32R), sb("vo_lo", [P, NH * P], F32R)

        xnT_hi, xnT_lo = sb("xnT_hi", [P, CW], F32R), sb("xnT_lo", [P, CW], F32R)
        cT_hi, cT_lo = sb("cT_hi", [P, CW], F32R), sb("cT_lo", [P, CW], F32R)
        cT_m = sb("cT_m", [P, CW + SEQ])
        q_T = sb("q_T", [P, BPC, NH, SEQ])
        v_o = [sb(f"v_o{i}", [P, NH, P]) for i in range(2)]
        sc_m = [sb(f"sc_m{i}", [P, 2, HP, SEQ]) for i in range(SRING)]
        prob = [sb(f"prob{i}", [P, HP, 2, SEQ]) for i in range(2)]
        nmax = [sb(f"nmax{i}", [P, 2 * HP]) for i in range(SRING)]
        esum = [sb(f"esum{i}", [P, 2 * HP]) for i in range(SRING)]
        rsum = [sb(f"rsum{i}", [P, 2 * HP]) for i in range(SRING)]
        prob_T = [sb(f"prob_T{i}", [P, NH, 2, SEQ]) for i in range(2)]

        x1_b2 = sb("x1_b2", [P, TPC, P])
        x1_T = sb("x1_T", [P, CW])
        hid = sb("hid", [P, NF, CW])
        z = x1_b2
        xm_T = sb("xm_T", [P, CW])
        y = x2 = ctx_all
        x_beta = x_all
        mT_hi, mT_lo = sb("mT_hi", [P, T], F32R), sb("mT_lo", [P, T], F32R)
        logits = sb("logits", [P, NT, NE])

        cen = [sb(f"cen{i}", [P, TPC, P]) for i in range(4)]
        stat = [sb(f"stat{i}", [P, TPC, 6]) for i in range(4)]
        mean_var = [sb(f"mean_var{i}", [P, TPC, 2]) for i in range(4)]
        var_eps = [sb(f"var_eps{i}", [P, TPC]) for i in range(4)]
        rstd = [sb(f"rstd{i}", [P, TPC]) for i in range(4)]
        rstd_g = [sb(f"rstd_g{i}", [P, TPC]) for i in range(4)]
        xn, x1, ffn_n, xm = cen
        b2_beta = sb("b2_beta", [P, P])

        we_hi = [sb(f"we_hi{i}", [P, 3 * P], F32R) for i in range(2)]
        we_lo = [sb(f"we_lo{i}", [P, 3 * P], F32R) for i in range(2)]
        we_hi += [w[:, 0:3 * P] for w in (xnT_hi, cT_hi)]
        we_lo += [w[:, 0:3 * P] for w in (xnT_lo, cT_lo)]
        comb = [wqk_in[:].rearrange("p a h k -> p (a h k)"), wvo_in[:].rearrange("p a h k -> p (a h k)")]
        wT_flat = wT[:].rearrange("p a h k -> p (a h k)").rearrange("p (n t) -> p n t", t=CW)
        silu, s_u, act = ([wT_flat[:, 2 * a + i, :] for i in range(2)] for a in range(3))
        act_hi = [w[:].rearrange("p h k -> p (h k)")[:, i * CW:(i + 1) * CW] for w in (qk_hi, qk_lo) for i in range(2)]
        act_lo = [w[:, i * CW:(i + 1) * CW] for w in (vo_hi, vo_lo) for i in range(2)]
        comb_dram = nc.dram_tensor("comb_dram", [2, P, P], F32, kind="Internal").ap()

        BATCH = [(0, NT // 2), (NT // 2, NT // 2)]
        lower = sb("lower", [P, NG, NG])
        top8 = sb("top8", [P, NT, 8])
        w_sum = sb("w_sum", [P, NT])
        w_inv = sb("w_inv", [P, NT])
        comb_w = sb("comb_w", [P, NT, NE])
        comb_T = sb("comb_T", [P, len(BATCH), P])
        q_flat = q_T[:].rearrange("p b h s -> p (b h s)")

        class Scratch:
            def __init__(self, b):
                self.n = n = BATCH[b][1]
                room, at = ((comb[0], 0), (q_flat, 0))[b]

                def take(width):
                    nonlocal at
                    at += n * width
                    return room[:, at - n * width:at].rearrange("p (t e) -> p t e", e=width)

                self.score, self.biased, self.kept_score, self.m_tmp = (take(NE) for _ in range(4))
                self.choice, self.taken = (take(NE + 8 - TOPK) for _ in range(2))
                self.pair_sum = take(NG * 6).rearrange("p t (g n) -> p t g n", n=6)
                self.g_score, self.g_less, self.g_rank = (take(NG) for _ in range(3))
                self.gg_a, self.gg_b = (take(NG * NG).rearrange("p t (g k) -> p t g k", k=NG) for _ in range(2))

        scratch = [Scratch(b) for b in range(len(BATCH))]

        bank = [es.enter_context(nc.psum_tensor(f"bank{i}", [P, CW], F32)) for i in range(8)]
        work = bank[0:3]
        sc_bank = bank[3:5]
        t_bank, av_bank, post_bank = bank[5], bank[6], bank[7]
        acc = [bank[0], bank[1], bank[2], bank[7]]
        h_bank, u_bank = [bank[3], bank[5]], [bank[4], bank[6]]

        ld_x0, ld_x, ld_c0, ld_c = sem("ld_x0"), sem("ld_x"), sem("ld_c0"), sem("ld_c")
        ld_mask, ld_small, ld_vec = sem("ld_mask"), sem("ld_small"), sem("ld_vec")
        ld_wq, ld_wk, ld_wv, ld_wo, ld_ffn = sem("ld_wq"), sem("ld_wk"), sem("ld_wv"), sem("ld_wo"), sem("ld_ffn")
        ld_exp = sem("ld_exp")
        const_step, ident_done, zero_done = sem("const_step"), sem("ident_done"), sem("zero_done")
        small_zero = sem("small_zero")
        small_turned, small_done = sem("small_turned"), sem("small_done")
        mask_done = sem("mask_done")
        w_turned = sem("w_turned")
        wT_done = [sem(f"wT_done{i}") for i in range(3)]
        fold_done = sem("fold_done")
        fold_hi, fold_lo = sem("fold_hi"), sem("fold_lo")
        stat_ready = [sem(f"stat_ready{i}") for i in range(4)]
        mean_var_ready = [sem(f"mean_var_ready{i}") for i in range(4)]
        var_ready = [sem(f"var_ready{i}") for i in range(4)]
        rstd_step = [sem(f"rstd_step{i}") for i in range(4)]
        rstd_ready = [sem(f"rstd_ready{i}") for i in range(4)]
        norm_ready = [sem(f"norm_ready{i}") for i in range(4)]
        b2_beta_ready, x2_ready = sem("b2_beta_ready"), sem("x2_ready")
        work_full = [sem(f"work_full{i}") for i in range(3)]
        work_free = [sem(f"work_free{i}") for i in range(3)]
        xnT_hi_ready = sem("xnT_hi_ready")
        cT_hi_ready, cT_lo_ready = sem("cT_hi_ready"), sem("cT_lo_ready")
        sc_full, sc_taken, max_ready = sem("sc_full"), sem("sc_taken"), sem("max_ready")
        sub_ready, exp_ready = sem("sub_ready"), sem("exp_ready")
        sum_ready, rsum_ready = sem("sum_ready"), sem("rsum_ready")
        prob_ready, t_full, prob_T_ready = sem("prob_ready"), sem("t_full"), sem("prob_T_ready")
        av_full, y_ready = sem("av_full"), sem("y_ready")
        post_full, post_free = sem("post_full"), sem("post_free")
        xm_full, mT_lo_ready = sem("xm_full"), sem("mT_lo_ready")
        logits_full, logits_ready = sem("logits_full"), sem("logits_ready")
        x1_b2_ready, x_beta_ready = sem("x1_b2_ready"), sem("x_beta_ready")
        mT_hi_ready, xm_T_ready = sem("mT_hi_ready"), sem("xm_T_ready")
        sigmoid_ready, route_step, route_done = sem("sigmoid_ready"), sem("route_step"), sem("route_done")
        comb_turned, comb_T_ready, comb_stored = sem("comb_turned"), sem("comb_T_ready"), sem("comb_stored")
        first_full, first_ready = sem("first_full"), sem("first_ready")
        comb_loaded = [sem(f"comb_loaded{i}") for i in range(2)]
        gu_hi_ready, gu_lo_ready = sem("gu_hi_ready"), sem("gu_lo_ready")
        dn_hi_ready, dn_lo_ready = sem("dn_hi_ready"), sem("dn_lo_ready")
        h_full, u_full, down_full = sem("h_full"), sem("u_full"), sem("down_full")
        silu_ready, s_u_ready, weighed_ready = sem("silu_ready"), sem("s_u_ready"), sem("weighed_ready")
        act_hi_ready, act_lo_ready = sem("act_hi_ready"), sem("act_lo_ready")
        acc_copied = [sem(f"acc_copied{i}") for i in range(CH)]
        out_turned, out_ready, stored = sem("out_turned"), sem("out_ready"), sem("stored")

        fold_bank = [bank[6], bank[7], bank[3], bank[4]]
        USES = 2 + NH + 2 * TPC
        per_slot = USES // 3
        assert USES % 3 == 0
        QUERY, VALUE = 2, 2 + NH

        def nth_use(c, k):
            return c * per_slot + (k // 3 + 1)

        FIRST = [(0, 0), (0, 1), (1, 0), (1, 1), (2, 0), (2, 1), (3, 0), (3, 1),
                 (0, 2), (1, 2), (0, 3), (1, 3), (2, 2), (2, 3), (3, 2), (3, 3)]
        DVE_WEIGHS = (3, 5, 7)
        POOL_LOW = (0, 1, 2, 3, 8, 9, 10, 11)
        LATER = [(i, c) for i in range(2) for c in range(CH)]

        def early(j):
            return isinstance(j, int) and j == 0

        def weighted(n):
            return not (isinstance(n, int) and n < FEW and FIRST[n][0] < NSH)

        def weighed_count(n):
            return n + 1 - (sum(not weighted(m) for m in range(n + 1)) if isinstance(n, int) else NSH * CH)

        POSTS = 4

        def post_count(c, k):
            return c * POSTS + k

        xm_bank = [work[2] if c == CH - 2 else post_bank for c in range(CH)]
        comb_bank = [work[2], post_bank]

        x_t = x.rearrange("b s d -> (b s) d").rearrange("(t p) d -> p t d", p=P)
        c_t = ctx_in.rearrange("b s d -> (b s) d").rearrange("(t p) d -> p t d", p=P)
        out_t = out.rearrange("b s d -> (b s) d").rearrange("(t p) d -> p t d", p=P)

        block = es.enter_context(nc.Block())

        @block.sync
        def _(sp):
            sp.dma_start(x_all[:, 0:TPC, :], x_t[:, 0:TPC, :]).then_inc(ld_x0, 16)
            sp.dma_start(small_in[0:NE, :], router_w).then_inc(ld_small, 16)
            sp.dma_start(small_in[NE:NE + NF, :], b1.rearrange("(j f) -> j f", f=P)).then_inc(ld_small, 16)
            sp.dma_start(wv_in, wv.rearrange("h d v -> d h v")).then_inc(ld_wv, 16)
            sp.dma_start(ctx_all[:, 0:TPC, :], c_t[:, 0:TPC, :]).then_inc(ld_c0, 16)
            sp.dma_start(wo_in, wo.rearrange("(h v) d -> v h d", v=P)).then_inc(ld_wo, 16)
            sp.dma_start(mask_row[:], mask.rearrange("b s -> (b s)").partition_broadcast(P)).then_inc(ld_mask, 16)
            sp.dma_start(x_all[:, TPC:, :], x_t[:, TPC:, :]).then_inc(ld_x, 16)
            sp.dma_start(ctx_all[:, TPC:, :], c_t[:, TPC:, :]).then_inc(ld_c, 16)
            sp.dma_start(gam[:], gamma.partition_broadcast(P)).then_inc(ld_vec, 16)
            sp.dma_start(bet[:], beta.partition_broadcast(P)).then_inc(ld_vec, 16)
            sp.dma_start(b2_row[:], b2.partition_broadcast(P)).then_inc(ld_vec, 16)
            sp.dma_start(bias_row[:], bias.partition_broadcast(P)).then_inc(ld_vec, 16)
            sp.dma_start(w1_in[:], w1).then_inc(ld_ffn, 16)
            sp.dma_start(w2_in[:], w2.rearrange("(j f) d -> f j d", f=P)).then_inc(ld_ffn, 16)
            for i, w in enumerate((sh_gate, sh_up)):
                sp.dma_start(w_exp[:, 0:NSH, i * P:(i + 1) * P],
                             w.rearrange("d (e f) -> d e f", f=P)).then_inc(ld_exp, 16)
            sp.dma_start(w_exp[:, 0:NSH, 2 * P:], sh_down.rearrange("(e f) d -> f e d", f=P)).then_inc(ld_exp, 16)
            sp.dma_start(w_exp[:, NSH:, 0:P], gate_w.rearrange("e d f -> d e f")).then_inc(ld_exp, 16)
            sp.dma_start(w_exp[:, NSH:, P:2 * P], up_w.rearrange("e d f -> d e f")).then_inc(ld_exp, 16)
            sp.dma_start(w_exp[:, NSH:, 2 * P:], down_w.rearrange("e f d -> f e d")).then_inc(ld_exp, 16)

            rows = comb_dram.rearrange("a n p -> (a n) p")
            by_expert = comb_dram.rearrange("a (t e) p -> e (a t) p", e=NE)

            def to_all(e, t0, tn):
                return by_expert[bass.ds(e, 1), t0:t0 + tn].rearrange("e t p -> (e t) p").partition_broadcast(P)

            for b, (t0, tn) in enumerate(BATCH):
                sp.wait_ge(comb_T_ready, b + 1)
                sp.dma_start(rows[t0 * NE:(t0 + tn) * NE], comb_T[0:tn * NE, b, :]).then_inc(comb_stored, 16)
                sp.wait_ge(comb_stored, 16 * (b + 1))
                for i in range(b, 2):
                    sp.dma_start(comb[i][:, t0 * P:(t0 + tn) * P].rearrange("p (t n) -> p t n", n=P),
                                 to_all(i, t0, tn)).then_inc(comb_loaded[i], 16)

            def load_combine(j, i, used):
                sp.wait_ge(weighed_ready, used)
                sp.dma_start(comb[i].rearrange("p (t n) -> p t n", n=P),
                             to_all(j * 2 + (i - NSH), 0, NT)).then_inc(comb_loaded[i], 16)

            for i in range(2):
                load_combine(2, i, weighed_count(FIRST.index((2 + i, CH - 1))))
            with sp.Fori(3, NX // 2) as j:
                load_combine(j, 0, weighed_count(j * STEPS - CH - 1))
                load_combine(j, 1, weighed_count(j * STEPS - 1))
            for c in range(CH):
                sp.wait_ge(out_ready, c + 1)
                sp.dma_start(out_t[:, c * TPC:(c + 1) * TPC, :],
                             x2[:, c * TPC:(c + 1) * TPC, :]).then_inc(stored, 16)
            sp.wait_ge(stored, 16 * CH)

        @block.gpsimd
        def _(pool):
            def inverse_root(n, c):
                pool.wait_ge(var_ready[n], c + 1)
                if n in (1, 2):
                    pool.tensor_tensor(rstd[n][:], var_eps[n][:], neg_half[:], ALU.pow).then_inc(rstd_step[n], 1)
                    pool.wait_ge(rstd_step[n], c + 1)
                    pool.tensor_scalar(rstd_g[n][:], rstd[n][:], gam[:, n - 1:n], None,
                                       ALU.mult).then_inc(rstd_ready[n], 1)
                else:
                    pool.tensor_tensor(rstd[n][:], var_eps[n][:], neg_half[:], ALU.pow).then_inc(rstd_ready[n], 1)

            def subtract_max(c, p):
                i = (c * TPC + p) % SRING
                pool.wait_ge(max_ready, c * TPC + (p + 1))
                pool.tensor_tensor(sc_m[i][:], sc_m[i][:],
                                   nmax[i][:].rearrange("p (b h) -> p b h", h=HP).unsqueeze(3)
                                   .to_broadcast([P, 2, HP, SEQ]), ALU.add).then_inc(sub_ready, 1)

            def normalise_probs(c, p):
                i = (c * TPC + p) % SRING
                pool.wait_ge(rsum_ready, c * TPC + (p + 1))
                if not (c == 0 and p < 2):
                    pool.wait_ge(t_full, c * TPC + (p - 1))
                pool.tensor_tensor(prob[p % 2][:].rearrange("p h b t -> p b h t"), sc_m[i][:],
                                   rsum[i][:].rearrange("p (b h) -> p b h", h=HP).unsqueeze(3)
                                   .to_broadcast([P, 2, HP, SEQ]), ALU.mult).then_inc(prob_ready, 1)

            def add_b2(c):
                pool.wait_ge(norm_ready[1], c + 1)
                if c:
                    pool.wait_ge(norm_ready[2], c)
                pool.tensor_tensor(x1_b2[:], x1[:], b2_beta[:].unsqueeze(1).to_broadcast([P, TPC, P]),
                                   ALU.add).then_inc(x1_b2_ready, 1)

            def add_beta(c):
                pool.wait_ge(norm_ready[0], c + 1)
                now = x_all[:, c * TPC:(c + 1) * TPC, :]
                pool.tensor_scalar(now, now, bet[:, 1:2], None, ALU.add).then_inc(x_beta_ready, 1)

            pool.memset(ident[:], 1.0).then_inc(const_step, 1)
            pool.wait_ge(const_step, 1)
            pool.affine_select(out=ident[:], in_=ident[:], compare_op=ALU.is_equal, fill=0.0, base=0,
                               pattern=[[1, P]], channel_multiplier=-1).then_inc(ident_done, 1)
            pool.memset(neg_half[:], -0.5).then_inc(const_step, 1)
            pool.wait_ge(const_step, 2)
            inverse_root(0, 0)
            pool.memset(small_T[:], 0.0).then_inc(small_zero, 1)
            pool.memset(cT_m[:, CW:], 0.0)
            pool.memset(lower[:], 1.0).then_inc(const_step, 1)
            for i in range(2):
                z_last = pool.memset(prob_T[i][:], 0.0)
            z_last.then_inc(zero_done, 1)
            pool.wait_ge(const_step, 3)
            pool.affine_select(out=lower[:], in_=lower[:], compare_op=ALU.is_ge, fill=0.0, base=-1,
                               pattern=[[1, NG], [-1, NG]], channel_multiplier=0).then_inc(const_step, 1)
            pool.wait_ge(ld_vec, 64)
            pool.tensor_scalar(b2_beta[:], b2_row[:], bet[:, 0:1], None, ALU.add).then_inc(b2_beta_ready, 1)
            pool.wait_ge(b2_beta_ready, 1)

            def split_lo(part, e, slot):
                a, b = (0, 2 * P) if part == "gu" else (2 * P, 3 * P)
                hi, lo = (gu_hi_ready, gu_lo_ready) if part == "gu" else (dn_hi_ready, dn_lo_ready)
                pool.wait_ge(hi, e + 1)
                pool.tensor_tensor(we_lo[slot][:, a:b], w_exp[:, bass.ds(e, 1), a:b].rearrange("p e n -> p (e n)"),
                                   we_hi[slot][:, a:b].bitcast(F32), ALU.subtract).then_inc(lo, 1)

            for c in range(CH + 1):
                now, last, before = c < CH, c >= 1, c >= 2
                if last:
                    normalise_probs(c - 1, 3)
                if before:
                    inverse_root(2, c - 2)
                if last and now:
                    add_beta(c - 1)
                if before and now:
                    for part in ("gu", "dn"):
                        split_lo(part, c - 2, c - 2)
                if c == CH:
                    for part in ("gu", "dn"):
                        split_lo(part, 2, 2)
                    add_beta(CH - 1)
                if before and now:
                    inverse_root(3, c - 2)
                if now:
                    subtract_max(c, 0)
                if last:
                    inverse_root(1, c - 1)
                if not now:
                    break
                subtract_max(c, 1)
                normalise_probs(c, 0)
                if last:
                    add_b2(c - 1)
                if c + 1 < CH:
                    inverse_root(0, c + 1)
                subtract_max(c, 2)
                normalise_probs(c, 1)
                normalise_probs(c, 2)
                subtract_max(c, 3)

            def weigh(j, k):
                n = j * STEPS + k
                i, c = (FIRST if early(j) else LATER)[k]
                pool.wait_ge(s_u_ready, n + 1)
                pool.wait_ge(act_lo_ready, n - 1)
                if early(j):
                    i -= NSH
                    if c == 0:
                        pool.wait_ge(comb_loaded[i], 16)
                    elif c >= CH // 2 and i == 0:
                        pool.wait_ge(first_ready, c - CH // 2 + 1)
                    elif c == CH // 2:
                        pool.wait_ge(comb_loaded[i], 32)
                elif c == 0:
                    pool.wait_ge(comb_loaded[i], (j + i) * 16)
                pool.tensor_tensor(act[k % 2], s_u[k % 2], comb[i][:, c * CW:(c + 1) * CW], ALU.mult
                                   ).then_inc(weighed_ready, 1)

            def experts(j, last):
                for k in range(STEPS):
                    if k == 0:
                        split_lo("gu", j * 2 + 1, 1)
                    if k == 3:
                        split_lo("dn", j * 2, 0)
                    if k == 4 and not last:
                        split_lo("gu", j * 2 + 2, 0)
                    if k == 5:
                        split_lo("dn", j * 2 + 1, 1)
                    if k not in DVE_WEIGHS:
                        weigh(j, k)

            def act_low(k):
                if k:
                    pool.wait_ge(act_lo_ready, k)
                pool.wait_ge(act_hi_ready, k + 1)
                pool.tensor_tensor(act_lo[k % 4], act[k % 2], act_hi[k % 4].bitcast(F32),
                                   ALU.subtract).then_inc(act_lo_ready, 1)

            def mT_low(c):
                pool.wait_ge(mT_hi_ready, c + 1)
                pool.tensor_tensor(mT_lo[:, bass.ts(c, CW)], xm_T[:], mT_hi[:, bass.ts(c, CW)].bitcast(F32),
                                   ALU.subtract).then_inc(mT_lo_ready, 1)

            for part in ("gu", "dn"):
                split_lo(part, 3, 3)
            act_low(0)
            inverse_root(3, CH - 2)
            act_low(1)
            add_b2(CH - 1)
            act_low(2)
            act_low(3)
            weigh(0, 4)
            inverse_root(2, CH - 1)
            weigh(0, 5)
            mT_low(CH - 2)
            inverse_root(3, CH - 1)
            weigh(0, 6)
            weigh(0, 7)
            for k in range(8, 12):
                act_low(k)
            weigh(0, 12)
            weigh(0, 13)
            split_lo("gu", 4, 0)
            weigh(0, 14)
            weigh(0, 15)

            with pool.Fori(2, NX // 2 - 1) as j:
                experts(j, False)
            experts(NX // 2 - 1, True)

        @block.scalar
        def _(a):
            a.dma_start(wqk_in[:, 0], wq.rearrange("h d k -> d h k")).then_inc(ld_wq, 16)
            a.dma_start(wqk_in[:, 1], wk.rearrange("h d k -> d h k")).then_inc(ld_wk, 16)

            def xnT_high(c):
                a.wait_ge(work_full[0], nth_use(c, 0))
                if c:
                    a.wait_ge(work_full[(VALUE - 1) % 3], nth_use(c - 1, VALUE - 1))
                a.copy(xnT_hi[:], work[0][:]).then_inc(xnT_hi_ready, 1)

            def cT_high(c):
                a.wait_ge(work_full[1], nth_use(c, 1))
                if c:
                    a.wait_ge(work_full[(USES - 1) % 3], nth_use(c - 1, USES - 1))
                a.copy(cT_hi[:], work[1][:]).then_inc(cT_hi_ready, 1)

            def query(c, h):
                k = QUERY + h
                a.wait_ge(work_full[k % 3], nth_use(c, k))
                if h == 0 and c:
                    a.wait_ge(sc_full, c * TPC)
                a.copy(q_T[:, :, h, :], work[k % 3][:].rearrange("p (b s) -> p b s", s=SEQ)
                       ).then_inc(work_free[k % 3], 1)

            def value(c, p):
                if not (c == 0 and p < 2):
                    a.wait_ge(av_full, c * TPC + (p - 1))
                for j in range(2):
                    k = VALUE + 2 * p + j
                    a.wait_ge(work_full[k % 3], nth_use(c, k))
                    a.copy(v_o[p % 2][:, j * HP:(j + 1) * HP, :].rearrange("p h d -> p (h d)"),
                           work[k % 3][:]).then_inc(work_free[k % 3], 1)

            def exponent(c, p):
                a.wait_ge(sub_ready, c * TPC + (p + 1))
                i = (c * TPC + p) % SRING
                a.activation(sc_m[i][:], sc_m[i][:], ACT.Exp).then_inc(exp_ready, 1)

            def spread(c, p):
                a.wait_ge(t_full, c * TPC + (p + 1))
                if not (c == 0 and p < 2):
                    a.wait_ge(av_full, c * TPC + (p - 1))
                for s in range(2):
                    rows = slice(s * SEQ, (s + 1) * SEQ)
                    last = a.copy(prob_T[p % 2][rows, :, s, :],
                                  t_bank[rows, :].rearrange("p (h s) -> p h s", s=SEQ))
                last.then_inc(prob_T_ready, 1)

            def turn_x1(c):
                a.wait_ge(post_full, c * POSTS + 1)
                a.activation(x1_T[:], post_bank[:], ACT.Identity, bias=bet[:, 0:1]).then_inc(post_free, 1)

            def hidden(c, j):
                a.wait_ge(post_full, c * POSTS + (2 + j))
                a.activation(hid[:, j, :], post_bank[:], ACT.Relu,
                             bias=small_T[:, NE + j:NE + j + 1]).then_inc(post_free, 1)

            def xm_high(c):
                a.wait_ge(xm_full, c + 1)
                if c:
                    a.wait_ge(mT_lo_ready, c)
                    a.wait_ge(logits_full, c)
                a.copy(xm_T[:], xm_bank[c][:]).then_inc(xm_T_ready, 1)
                a.wait_ge(xm_T_ready, c + 1)
                a.copy(mT_hi[:, bass.ts(c, CW)], xm_T[:]).then_inc(mT_hi_ready, 1)

            def fold_high(i):
                a.wait_ge(fold_done, i + 1)
                hi, half = (qk_hi, qk_hi, vo_hi, vo_hi)[i], i % 2
                dst = hi[:, half * HP:(half + 1) * HP, :].rearrange("p h d -> p (h d)") if i < 2 else \
                    hi[:, half * CW:(half + 1) * CW]
                a.copy(dst, fold_bank[i][:]).then_inc(fold_hi, 1)

            def router_sigmoid(b):
                t0, tn = BATCH[b]
                a.wait_ge(logits_ready, (t0 + tn) // TPC)
                if b == 0:
                    a.activation(scratch[b].score, logits[:, t0:t0 + tn, :], ACT.Exp, scale=-1.0
                                 ).then_inc(sigmoid_ready, 1)
                else:
                    a.activation(scratch[b].score, logits[:, t0:t0 + tn, :], ACT.Sigmoid).then_inc(sigmoid_ready, 1)

            def split_hi(part, e, slot):
                a0, b0 = (0, 2 * P) if part == "gu" else (2 * P, 3 * P)
                hi = gu_hi_ready if part == "gu" else dn_hi_ready
                a.copy(we_hi[slot][:, a0:b0],
                       w_exp[:, bass.ds(e, 1), a0:b0].rearrange("p e n -> p (e n)")).then_inc(hi, 1)

            for i in range(3):
                a.wait_ge(w_turned, 2 * i + 1)
                a.copy(wT[:, i, 0:HP, :].rearrange("p h d -> p (h d)"), bank[2 * i][:]).then_inc(wT_done[i], 1)
            for i in range(2):
                fold_high(i)

            for c in range(CH + 1):
                now, last, before = c < CH, c >= 1, c >= 2
                if last:
                    spread(c - 1, 2)
                if now:
                    xnT_high(c)
                    cT_high(c)
                if c == 0:
                    fold_high(2)
                    fold_high(3)
                    a.wait_ge(small_turned, 1)
                    a.wait_ge(small_zero, 1)
                    a.copy(small_T[:, 0:NE + NF], t_bank[:, 0:NE + NF]).then_inc(small_done, 1)
                    a.wait_ge(small_done, 1)
                    a.wait_ge(zero_done, 1)
                if now:
                    query(c, 0)
                    query(c, 1)
                if c == CH:
                    for part in ("gu", "dn"):
                        split_hi(part, 3, 3)
                if last:
                    spread(c - 1, 3)
                if not now:
                    break
                query(c, 2)
                query(c, 3)
                query(c, 4)
                query(c, 5)
                query(c, 6)
                query(c, 7)
                if before:
                    xm_high(c - 2)
                value(c, 0)
                exponent(c, 0)
                value(c, 1)
                exponent(c, 1)
                if c == CH - 1:
                    router_sigmoid(0)
                if c == 1:
                    a.wait_ge(ld_vec, 64)
                if last:
                    turn_x1(c - 1)
                spread(c, 0)
                exponent(c, 2)
                if last:
                    hidden(c - 1, 0)
                value(c, 2)
                if last:
                    hidden(c - 1, 1)
                spread(c, 1)
                exponent(c, 3)
                value(c, 3)
                if c:
                    if c == 1:
                        a.wait_ge(ld_exp, 6 * 16)
                    for part in ("gu", "dn"):
                        split_hi(part, c - 1, c - 1)

            def gate(j, k):
                n = j * STEPS + k
                a.wait_ge(h_full, n + 1)
                if not (early(j) and k < 2):
                    a.wait_ge(s_u_ready, n - 1)
                a.activation(silu[k % 2], h_bank[k % 2][:], ACT.Silu).then_inc(silu_ready, 1)

            def act_high(j, k):
                n = j * STEPS + k
                if weighted(n):
                    a.wait_ge(weighed_ready, weighed_count(n))
                else:
                    a.wait_ge(s_u_ready, n + 1)
                if not (early(j) and k < 4):
                    a.wait_ge(down_full, n - 3)
                a.copy(act_hi[k % 4], act[k % 2]).then_inc(act_hi_ready, 1)

            def experts(j, last):
                for k in range(STEPS):
                    if k == 0:
                        a.wait_ge(u_full, j * STEPS)
                        split_hi("gu", j * 2 + 1, 1)
                    if k == 3:
                        a.wait_ge(down_full, j * STEPS - 1)
                        split_hi("dn", j * 2, 0)
                    if k == 4 and not last:
                        a.wait_ge(u_full, j * STEPS + CH)
                        split_hi("gu", j * 2 + 2, 0)
                    if k == 5:
                        a.wait_ge(down_full, j * STEPS)
                        split_hi("dn", j * 2 + 1, 1)
                    gate(j, k)
                    act_high(j, k - 1)

            def first_weights(c):
                a.wait_ge(first_full, c - CH // 2 + 1)
                a.copy(comb[0][:, c * CW:(c + 1) * CW], post_bank[:]).then_inc(first_ready, 1)

            gate(0, 0)
            gate(0, 1)
            act_high(0, 0)
            gate(0, 2)
            turn_x1(CH - 1)
            act_high(0, 1)
            gate(0, 3)
            hidden(CH - 1, 0)
            act_high(0, 2)
            hidden(CH - 1, 1)
            gate(0, 4)
            act_high(0, 3)
            gate(0, 5)
            act_high(0, 4)
            xm_high(CH - 2)
            gate(0, 6)
            act_high(0, 5)
            gate(0, 7)
            act_high(0, 6)
            xm_high(CH - 1)
            gate(0, 8)
            router_sigmoid(1)
            act_high(0, 7)
            for k in range(9, 13):
                gate(0, k)
                act_high(0, k - 1)
            gate(0, 13)
            first_weights(CH // 2)
            gate(0, 14)
            first_weights(CH // 2 + 1)
            act_high(0, 12)
            a.wait_ge(u_full, FIRST.index((0, CH - 1)) + 1)
            split_hi("gu", 4, 0)
            gate(0, 15)
            act_high(0, 13)
            act_high(0, 14)

            with a.Fori(2, NX // 2 - 1) as j:
                experts(j, False)
            experts(NX // 2 - 1, True)
            act_high(NX // 2, -1)
            for c in range(0, CH, 2):
                a.wait_ge(down_full, NX * CH - CH + c + 1)
                a.copy(q_flat[:, c * CW:(c + 1) * CW], acc[c][:]).then_inc(acc_copied[c], 1)

        @block.vector
        def _(v):
            def statistics(n, c, src):
                for t in range(TPC):
                    last = v.bn_stats(stat[n][:, t, :], src[:, t, :])
                last.then_inc(stat_ready[n], 1)
                v.wait_ge(stat_ready[n], c + 1)
                for t in range(TPC):
                    last = v.bn_aggr(mean_var[n][:, t, :], stat[n][:, t, :])
                last.then_inc(mean_var_ready[n], 1)
                v.wait_ge(mean_var_ready[n], c + 1)
                v.tensor_scalar(var_eps[n][:], mean_var[n][:, :, 1], EPS_ATTN if n in (1, 2) else EPS_IN, None,
                                ALU.add).then_inc(var_ready[n], 1)

            def normalise(n, c, src):
                v.wait_ge(rstd_ready[n], c + 1)
                by = rstd_g if n in (1, 2) else rstd
                for t in range(TPC):
                    last = v.tensor_scalar(cen[n][:, t, :], src[:, t, :], mean_var[n][:, t, 0:1], by[n][:, t:t + 1],
                                           ALU.subtract, ALU.mult)
                last.then_inc(norm_ready[n], 1)

            def tokens(t, c):
                return t[:, c * TPC:(c + 1) * TPC, :]

            def residual(c):
                normalise(2, c, z)
                v.wait_ge(norm_ready[2], c + 1)
                v.wait_ge(x_beta_ready, c + 1)
                v.tensor_tensor(tokens(x2, c), ffn_n[:], tokens(x_beta, c), ALU.add).then_inc(x2_ready, 1)
                v.wait_ge(x2_ready, c + 1)

            def xnT_low(c):
                v.wait_ge(xnT_hi_ready, c + 1)
                v.tensor_tensor(xnT_lo[:], work[0][:], xnT_hi[:].bitcast(F32), ALU.subtract).then_inc(work_free[0], 1)

            def cT_low(c):
                v.wait_ge(cT_hi_ready, c + 1)
                v.tensor_tensor(cT_lo[:], work[1][:], cT_hi[:].bitcast(F32), ALU.subtract).then_inc(cT_lo_ready, 1)
                if c:
                    v.wait_ge(sc_full, c * TPC)
                v.tensor_tensor(cT_m[:, 0:CW], work[1][:], mask_row[:, bass.ts(c, CW)],
                                ALU.mult).then_inc(work_free[1], 1)
                v.tensor_scalar(mask_add[:], mask_row[:, bass.ts(c, CW)], -1.0, BIG, ALU.add,
                                ALU.mult).then_inc(mask_done, 1)

            def mask_and_max(c, p):
                i = (c * TPC + p) % SRING
                if c * TPC + p >= SRING:
                    v.wait_ge(prob_ready, c * TPC + p - SRING + 1)
                v.wait_ge(sc_full, c * TPC + (p + 1))
                v.wait_ge(mask_done, c + 1)
                for s in range(2):
                    last = v.tensor_tensor(
                        sc_m[i][:, s], sc_bank[s][:].rearrange("p (h t) -> p h t", t=P)[:, :, 0:SEQ],
                        mask_add[:, (2 * p + s) * SEQ:(2 * p + s + 1) * SEQ].unsqueeze(1)
                        .to_broadcast([P, HP, SEQ]), ALU.add)
                last.then_inc(sc_taken, 1)
                v.wait_ge(sc_taken, c * TPC + (p + 1))
                v.tensor_reduce(nmax[i][:].rearrange("p (b h) -> p b h", h=HP), sc_m[i][:], AX.X, ALU.max,
                                negate=True).then_inc(max_ready, 1)

            def sum_of_exp(c, p):
                i = (c * TPC + p) % SRING
                v.wait_ge(exp_ready, c * TPC + (p + 1))
                v.tensor_reduce(esum[i][:].rearrange("p (b h) -> p b h", h=HP), sc_m[i][:], AX.X,
                                ALU.add).then_inc(sum_ready, 1)
                v.wait_ge(sum_ready, c * TPC + (p + 1))
                v.reciprocal(rsum[i][:], esum[i][:]).then_inc(rsum_ready, 1)

            def add_ctx(c, p):
                v.wait_ge(av_full, c * TPC + (p + 1))
                tile = y[:, bass.ds(c * TPC + p, 1), :].rearrange("p o d -> p (o d)")
                v.tensor_tensor(tile, av_bank[:, 0:P], tile, ALU.add).then_inc(y_ready, 1)

            def add_ffn(c):
                v.wait_ge(post_full, c * POSTS + 4)
                v.wait_ge(x1_b2_ready, c + 1)
                v.tensor_tensor(z[:], post_bank[:].rearrange("p (t d) -> p t d", d=P), x1_b2[:],
                                ALU.add).then_inc(post_free, 1)
                v.wait_ge(post_free, post_count(c, 4))

            def mT_low(c):
                v.wait_ge(mT_hi_ready, c + 1)
                v.tensor_tensor(mT_lo[:, bass.ts(c, CW)], xm_T[:], mT_hi[:, bass.ts(c, CW)].bitcast(F32),
                                ALU.subtract).then_inc(mT_lo_ready, 1)

            def take_logits(c):
                v.wait_ge(logits_full, c + 1)
                v.tensor_copy(logits[:, bass.ts(c, TPC), :],
                              xm_bank[c][:].rearrange("p (t n) -> p t n", n=P)[:, :, 0:NE]).then_inc(logits_ready, 1)

            def fold_low(i):
                v.wait_ge(fold_hi, i + 1)
                half = i % 2
                dst, src = (w[:, half * HP:(half + 1) * HP, :].rearrange("p h d -> p (h d)") if i < 2 else
                            w[:, half * CW:(half + 1) * CW] for w in ((qk_lo, qk_hi) if i < 2 else (vo_lo, vo_hi)))
                v.tensor_tensor(dst, fold_bank[i][:], src.bitcast(F32), ALU.subtract).then_inc(fold_lo, 1)

            v.wait_ge(ld_x0, 16)
            statistics(0, 0, tokens(x_all, 0))
            for i in range(2):
                v.wait_ge(w_turned, 2 * i + 2)
                v.tensor_copy(wT[:, i, HP:, :].rearrange("p h d -> p (h d)"), bank[2 * i + 1][:]
                              ).then_inc(wT_done[i], 1)
            v.wait_ge(w_turned, 6)
            v.tensor_copy(wT[:, 2, HP:, :].rearrange("p h d -> p (h d)"), bank[5][:]).then_inc(wT_done[2], 1)
            normalise(0, 0, tokens(x_all, 0))
            for i in range(2):
                fold_low(i)
            v.wait_ge(ld_mask, 16)
            v.wait_ge(ld_c0, 16)

            steps = [0]

            def done(ins):
                steps[0] += 1
                ins.then_inc(route_step, 1)
                v.wait_ge(route_step, steps[0])

            def by_token(t, b, n):
                t0, tn = BATCH[b]
                return t[:, t0:t0 + tn].unsqueeze(2).to_broadcast([P, tn, n])

            def bias_scores(b):
                r = scratch[b]
                v.wait_ge(sigmoid_ready, b + 1)
                if b == 0:
                    done(v.tensor_scalar(r.m_tmp, r.score, 1.0, None, ALU.add))
                    done(v.reciprocal(r.score, r.m_tmp))
                v.memset(r.choice[:, :, NE:], MARK)
                done(v.tensor_tensor(r.biased, r.score, bias_row[:].unsqueeze(1).to_broadcast([P, r.n, NE]), ALU.add))

            def group_scores(b):
                r = scratch[b]
                s4 = r.biased.rearrange("p t (g n) -> p t g n", n=EPG)
                v.tensor_tensor(r.pair_sum[:, :, :, 0:3], s4[:, :, :, 0:3], s4[:, :, :, 1:4], ALU.add)
                v.tensor_tensor(r.pair_sum[:, :, :, 3:5], s4[:, :, :, 0:2], s4[:, :, :, 2:4], ALU.add)
                done(v.tensor_tensor(r.pair_sum[:, :, :, 5:6], s4[:, :, :, 0:1], s4[:, :, :, 3:4], ALU.add))
                done(v.tensor_reduce(r.g_score, r.pair_sum, AX.X, ALU.max))

            def keep_groups(b):
                r = scratch[b]
                mine = r.g_score.unsqueeze(3).to_broadcast([P, r.n, NG, NG])
                other = r.g_score.unsqueeze(2).to_broadcast([P, r.n, NG, NG])
                before = lower[:].unsqueeze(1).to_broadcast([P, r.n, NG, NG])
                if b == 0:
                    v.wait_ge(const_step, 4)
                v.tensor_tensor(r.gg_a, other, mine, ALU.is_gt)
                done(v.tensor_tensor(r.gg_b, other, mine, ALU.is_equal))
                done(v.tensor_tensor(r.gg_b, r.gg_b, before, ALU.mult))
                done(v.tensor_tensor(r.gg_a, r.gg_a, r.gg_b, ALU.add))
                done(v.tensor_reduce(r.g_rank, r.gg_a, AX.X, ALU.add))
                drop = r.g_rank.unsqueeze(3).to_broadcast([P, r.n, NG, EPG])
                less = r.g_less.unsqueeze(3).to_broadcast([P, r.n, NG, EPG])
                v.tensor_scalar(r.g_less, r.g_rank, 1.5, -1.0, ALU.is_gt, ALU.mult)
                done(v.scalar_tensor_tensor(r.m_tmp.rearrange("p t (g n) -> p t g n", n=EPG), drop, 1.5,
                                            r.biased.rearrange("p t (g n) -> p t g n", n=EPG), ALU.is_lt, ALU.mult))
                done(v.tensor_tensor(r.choice[:, :, 0:NE].rearrange("p t (g n) -> p t g n", n=EPG),
                                     r.m_tmp.rearrange("p t (g n) -> p t g n", n=EPG), less, ALU.add))

            def keep_experts(b):
                r = scratch[b]
                t0, tn = BATCH[b]
                for t in range(tn):
                    last = v.max(top8[:, t0 + t, :], r.choice[:, t, 0:NE])
                done(last)
                done(v.memset(top8[:, t0:t0 + tn, TOPK:], MARK))
                for t in range(tn):
                    last = v.match_replace(r.taken[:, t, :], top8[:, t0 + t, :], r.choice[:, t, :], TAKEN)
                done(last)

            def combine(b):
                r = scratch[b]
                t0, tn = BATCH[b]
                total = w_sum[:, t0:t0 + tn]
                done(v.scalar_tensor_tensor(r.kept_score, r.taken[:, :, 0:NE], TAKEN, r.score,
                                            ALU.is_equal, ALU.mult))
                done(v.tensor_reduce(total, r.kept_score, AX.X, ALU.add))
                done(v.tensor_scalar(total, total, 1e-20, None, ALU.add))
                done(v.reciprocal(w_inv[:, t0:t0 + tn], total))
                v.scalar_tensor_tensor(comb_w[:, t0:t0 + tn, :], r.kept_score, ROUTE_SCALE, by_token(w_inv, b, NE),
                                       ALU.mult, ALU.mult).then_inc(route_done, 1)

            def take_combine(b):
                rows = BATCH[b][1] * NE
                v.wait_ge(comb_turned, b + 1)
                v.tensor_copy(comb_T[0:rows, b, :], comb_bank[b][0:rows, 0:P]).then_inc(comb_T_ready, 1)

            for c in range(CH + 1):
                now, last, before = c < CH, c >= 1, c >= 2
                if last:
                    sum_of_exp(c - 1, 3)
                if before:
                    add_ffn(c - 2)
                if now:
                    xnT_low(c)
                    cT_low(c)
                if before:
                    statistics(2, c - 2, z)
                if last:
                    add_ctx(c - 1, 2)
                if c == 0:
                    fold_low(2)
                    fold_low(3)
                if c == CH:
                    combine(0)
                    residual(c - 2)
                    add_ctx(c - 1, 3)
                    v.wait_ge(y_ready, c * TPC)
                    statistics(1, c - 1, tokens(y, c - 1))
                    break
                if before:
                    residual(c - 2)
                    statistics(3, c - 2, tokens(x2, c - 2))
                    normalise(3, c - 2, tokens(x2, c - 2))
                if last:
                    add_ctx(c - 1, 3)
                mask_and_max(c, 0)
                if last:
                    v.wait_ge(y_ready, c * TPC)
                    statistics(1, c - 1, tokens(y, c - 1))
                if before:
                    mT_low(c - 2)
                mask_and_max(c, 1)
                if before:
                    take_logits(c - 2)
                if last:
                    normalise(1, c - 1, tokens(y, c - 1))
                sum_of_exp(c, 0)
                if c == 0:
                    v.wait_ge(ld_x, 16)
                    v.wait_ge(ld_c, 16)
                if c + 1 < CH:
                    statistics(0, c + 1, tokens(x_all, c + 1))
                else:
                    bias_scores(0)
                    group_scores(0)
                mask_and_max(c, 2)
                sum_of_exp(c, 1)
                if c + 1 < CH:
                    normalise(0, c + 1, tokens(x_all, c + 1))
                sum_of_exp(c, 2)
                mask_and_max(c, 3)
                add_ctx(c, 0)
                if c + 1 == CH:
                    keep_groups(0)
                add_ctx(c, 1)
                if c + 1 == CH:
                    keep_experts(0)

            def gate_up(j, k):
                n = j * STEPS + k
                v.wait_ge(silu_ready, n + 1)
                v.wait_ge(u_full, n + 1)
                if not weighted(n):
                    if k >= 2:
                        v.wait_ge(act_lo_ready, n - 1)
                    v.tensor_tensor(act[k % 2], u_bank[k % 2][:], silu[k % 2], ALU.mult).then_inc(s_u_ready, 1)
                    return
                if weighted(n - 2):
                    v.wait_ge(weighed_ready, weighed_count(n - 2))
                v.tensor_tensor(s_u[k % 2], u_bank[k % 2][:], silu[k % 2], ALU.mult).then_inc(s_u_ready, 1)

            def act_low(j, k):
                n = j * STEPS + k
                if early(j) and k - 1 in POOL_LOW:
                    v.wait_ge(act_lo_ready, k)
                v.wait_ge(act_hi_ready, n + 1)
                v.tensor_tensor(act_lo[k % 4], act[k % 2], act_hi[k % 4].bitcast(F32),
                                ALU.subtract).then_inc(act_lo_ready, 1)

            def weigh(j, k):
                n = j * STEPS + k
                i, c = LATER[k]
                v.wait_ge(s_u_ready, n + 1)
                v.tensor_tensor(act[k % 2], s_u[k % 2], comb[i][:, c * CW:(c + 1) * CW],
                                ALU.mult).then_inc(weighed_ready, 1)

            gate_up(0, 0)
            take_combine(0)
            normalise(1, CH - 1, tokens(y, CH - 1))
            gate_up(0, 1)
            statistics(3, CH - 2, tokens(x2, CH - 2))
            gate_up(0, 2)
            normalise(3, CH - 2, tokens(x2, CH - 2))
            gate_up(0, 3)
            gate_up(0, 4)
            add_ffn(CH - 1)
            statistics(2, CH - 1, z)
            gate_up(0, 5)
            act_low(0, 4)
            residual(CH - 1)
            statistics(3, CH - 1, tokens(x2, CH - 1))
            gate_up(0, 6)
            normalise(3, CH - 1, tokens(x2, CH - 1))
            take_logits(CH - 2)
            act_low(0, 5)
            gate_up(0, 7)
            act_low(0, 6)
            gate_up(0, 8)
            take_logits(CH - 1)
            mT_low(CH - 1)
            bias_scores(1)
            group_scores(1)
            act_low(0, 7)
            gate_up(0, 9)
            keep_groups(1)
            gate_up(0, 10)
            keep_experts(1)
            gate_up(0, 11)
            combine(1)
            take_combine(1)
            gate_up(0, 12)
            gate_up(0, 13)
            gate_up(0, 14)
            act_low(0, 12)
            gate_up(0, 15)
            act_low(0, 13)
            act_low(0, 14)

            with v.Fori(2, NX // 2) as j:
                for k in range(STEPS):
                    gate_up(j, k)
                    act_low(j, k - 1)
                    if k in DVE_WEIGHS:
                        weigh(j, k)
            act_low(NX // 2, -1)
            for c in range(1, CH, 2):
                v.wait_ge(down_full, NX * CH - CH + c + 1)
                v.tensor_copy(q_flat[:, c * CW:(c + 1) * CW], acc[c][:]).then_inc(acc_copied[c], 1)
            for c in range(CH):
                v.wait_ge(out_turned, c + 1)
                v.tensor_tensor(tokens(x2, c), (h_bank + u_bank)[c][:].rearrange("p (t d) -> p t d", d=P),
                                tokens(x2, c), ALU.add).then_inc(out_ready, 1)

        @block.tensor
        def _(pe):
            def three(dst, w_hi, w_lo, m_hi, m_lo, start, stop):
                pe.matmul(dst, w_hi, m_hi, start=start, stop=False)
                pe.matmul(dst, w_hi, m_lo, start=False, stop=False)
                return pe.matmul(dst, w_lo, m_hi, start=False, stop=stop)

            def work_bank(c, k):
                if not (c == 0 and k < 3):
                    pe.wait_ge(work_free[k % 3], nth_use(c, k) - 1)
                return work[k % 3]

            def turn_xn(c):
                w = work_bank(c, 0)
                pe.wait_ge(norm_ready[0], c + 1)
                for t in range(TPC):
                    last = pe.transpose(w[:, t * P:(t + 1) * P], xn[:, t, :], ident[:])
                last.then_inc(work_full[0], 1)

            def turn_ctx(c):
                w = work_bank(c, 1)
                if c == 0:
                    pe.wait_ge(ld_c0, 16)
                if c == 1:
                    pe.wait_ge(ld_c, 16)
                for t in range(TPC):
                    last = pe.transpose(w[:, t * P:(t + 1) * P], ctx_all[:, c * TPC + t, :], ident[:])
                last.then_inc(work_full[1], 1)

            def queries(c, heads):
                pe.wait_ge(work_free[0], nth_use(c, 0))
                for h in heads:
                    k = QUERY + h
                    w = work_bank(c, k)
                    three(w[:], qk_hi[:, h, :], qk_lo[:, h, :], xnT_hi[:], xnT_lo[:], True, True
                          ).then_inc(work_full[k % 3], 1)

            def values(c, p):
                if p == 0:
                    pe.wait_ge(cT_lo_ready, c + 1)
                tok = slice(p * P, (p + 1) * P)
                for j in range(2):
                    k = VALUE + 2 * p + j
                    w = work_bank(c, k)
                    cols = slice(j * CW, (j + 1) * CW)
                    three_moving(w[:], cT_hi[:, tok], cT_lo[:, tok], vo_hi[:, cols], vo_lo[:, cols]
                                 ).then_inc(work_full[k % 3], 1)

            def three_moving(dst, w_hi, w_lo, m_hi, m_lo):
                return three(dst, w_hi, w_lo, m_hi, m_lo, True, True)

            def scores(c, p):
                if p == 0:
                    for k in range(VALUE - 3, VALUE):
                        pe.wait_ge(work_free[k % 3], nth_use(c, k))
                    pe.wait_ge(work_free[1], nth_use(c, 1))
                if not (c == 0 and p == 0):
                    pe.wait_ge(sc_taken, c * TPC + p)
                for s in range(2):
                    b = 2 * p + s
                    for hp in range(HP):
                        last = pe.matmul(sc_bank[s][:, hp * P:(hp + 1) * P],
                                         q_T[:, b, 2 * hp:2 * hp + 2, :].rearrange("p h s -> p (h s)"),
                                         cT_m[:, b * SEQ:b * SEQ + P], start=True, stop=True)
                last.then_inc(sc_full, 1)

            def turn_probs(c, p):
                pe.wait_ge(prob_ready, c * TPC + (p + 1))
                if not (c == 0 and p == 0):
                    pe.wait_ge(prob_T_ready, c * TPC + p)
                for hp in range(HP):
                    last = pe.transpose(t_bank[:, hp * P:(hp + 1) * P],
                                        prob[p % 2][:, hp, :, :].rearrange("p b t -> p (b t)"), ident[:])
                last.then_inc(t_full, 1)

            def attend(c, p):
                pe.wait_ge(prob_T_ready, c * TPC + (p + 1))
                for j in range(2):
                    k = VALUE + 2 * p + j
                    pe.wait_ge(work_free[k % 3], nth_use(c, k))
                if not (c == 0 and p == 0):
                    pe.wait_ge(y_ready, c * TPC + p)
                for h in range(NH):
                    last = pe.matmul(av_bank[:, 0:P], prob_T[p % 2][:, h, :, :].rearrange("p b s -> p (b s)"),
                                     v_o[p % 2][:, h, :], start=(h == 0), stop=(h == NH - 1))
                last.then_inc(av_full, 1)

            def post_bank_for(c, k):
                pe.wait_ge(post_free, post_count(c, k))

            def turn_x1(c):
                pe.wait_ge(norm_ready[1], c + 1)
                if 0 < c < CH - 1:
                    pe.wait_ge(logits_ready, c)
                if c == CH - 1:
                    post_bank_for(c, 0)
                for t in range(TPC):
                    last = pe.transpose(post_bank[:, t * P:(t + 1) * P], x1[:, t, :], ident[:])
                last.then_inc(post_full, 1)

            def ffn_up(c, j):
                post_bank_for(c, 1 + j)
                pe.matmul(post_bank[:], w1_in[:, j * P:(j + 1) * P], x1_T[:],
                          start=True, stop=True).then_inc(post_full, 1)

            def ffn_down(c):
                post_bank_for(c, 3)
                for t in range(TPC):
                    for j in range(NF):
                        last = pe.matmul(post_bank[:, t * P:(t + 1) * P], hid[:, j, t * P:(t + 1) * P],
                                         w2_in[:, j, :], start=(j == 0), stop=(j == NF - 1))
                last.then_inc(post_full, 1)

            def turn_xm(c):
                if c == CH - 2:
                    pe.wait_ge(work_free[2], nth_use(CH - 1, USES - 1))
                    pe.wait_ge(comb_T_ready, 1)
                else:
                    post_bank_for(c, POSTS)
                pe.wait_ge(norm_ready[3], c + 1)
                for t in range(TPC):
                    last = pe.transpose(xm_bank[c][:, t * P:(t + 1) * P], xm[:, t, :], ident[:])
                last.then_inc(xm_full, 1)

            def route(c):
                pe.wait_ge(xm_T_ready, c + 1)
                for t in range(TPC):
                    last = pe.matmul(xm_bank[c][:, t * P:(t + 1) * P], xm_T[:, t * P:(t + 1) * P], small_T[:],
                                     start=True, stop=True)
                last.then_inc(logits_full, 1)

            pe.wait_ge(ident_done, 1)
            for i, ready in enumerate((ld_wq, ld_wk, ld_wv)):
                pe.wait_ge(ready, 16)
                for half in range(2):
                    for h in range(HP):
                        src = wqk_in[:, i, half * HP + h, :] if i < 2 else wv_in[:, half * HP + h, :]
                        last = pe.transpose(bank[2 * i + half][:, h * P:(h + 1) * P], src, ident[:])
                    last.then_inc(w_turned, 1)
            for i in range(2):
                pe.wait_ge(wT_done[i], 2)
            for half in range(2):
                for h in range(HP):
                    hh = half * HP + h
                    last = pe.matmul(fold_bank[half][:, h * P:(h + 1) * P], wT[:, 0, hh, :], wT[:, 1, hh, :],
                                     start=True, stop=True)
                last.then_inc(fold_done, 1)

            def fold_values():
                pe.wait_ge(wT_done[2], 2)
                pe.wait_ge(ld_wo, 16)
                for half in range(2):
                    for h in range(HP):
                        hh = half * HP + h
                        last = pe.matmul(fold_bank[2 + half][:, h * P:(h + 1) * P], wT[:, 2, hh, :], wo_in[:, hh, :],
                                         start=True, stop=True)
                    last.then_inc(fold_done, 1)
                pe.wait_ge(ld_small, 32)
                pe.transpose(t_bank[:, 0:NE + NF], small_in[:], ident[0:NE + NF, 0:NE + NF]).then_inc(small_turned, 1)

            for c in range(CH + 1):
                now, last, before = c < CH, c >= 1, c >= 2
                if now:
                    turn_xn(c)
                    turn_ctx(c)
                if last:
                    attend(c - 1, 2)
                if c == 0:
                    fold_values()
                    pe.wait_ge(fold_lo, 2)
                if now:
                    queries(c, range(0, 2))
                if last:
                    turn_probs(c - 1, 3)
                if now:
                    queries(c, range(2, NH))
                if c == 0:
                    pe.wait_ge(fold_lo, 4)
                    pe.wait_ge(small_done, 1)
                    pe.wait_ge(zero_done, 1)
                    pe.wait_ge(ld_ffn, 32)
                if last and now:
                    attend(c - 1, 3)
                if not now:
                    break
                if c == 0:
                    values(c, 0)
                scores(c, 0)
                if c:
                    values(c, 0)
                if before:
                    turn_xm(c - 2)
                scores(c, 1)
                if before:
                    route(c - 2)
                values(c, 1)
                scores(c, 2)
                if last:
                    turn_x1(c - 1)
                values(c, 2)
                turn_probs(c, 0)
                if last:
                    ffn_up(c - 1, 0)
                scores(c, 3)
                attend(c, 0)
                if last:
                    ffn_up(c - 1, 1)
                turn_probs(c, 1)
                values(c, 3)
                attend(c, 1)
                turn_probs(c, 2)
                if last:
                    ffn_down(c - 1)

            def turn_combine(b):
                t0, tn = BATCH[b]
                pe.wait_ge(route_done, b + 1)
                if b == 0:
                    pe.wait_ge(work_free[2], nth_use(CH - 1, USES - 1))
                else:
                    pe.wait_ge(logits_ready, CH)
                pe.transpose(comb_bank[b][0:tn * NE, 0:P], comb_w[:, t0:t0 + tn, :].rearrange("p t e -> p (t e)"),
                             ident[:]).then_inc(comb_turned, 1)

            def first_weights(c):
                for t in range(TPC):
                    row = (c * TPC + t - BATCH[1][0]) * NE
                    last = pe.matmul(post_bank[:, t * P:(t + 1) * P], ident[:, row:row + 1].to_broadcast([P, P]),
                                     comb_T[:, 1, :], start=True, stop=True)
                last.then_inc(first_full, 1)

            def up(j, k):
                n = j * STEPS + k
                i, c = (FIRST if early(j) else LATER)[k]
                if c == 0:
                    pe.wait_ge(gu_lo_ready, j * 2 + (i + 1))
                if early(j) and i == 0:
                    pe.wait_ge(mT_lo_ready, c + 1)
                cols = slice(c * CW, (c + 1) * CW)
                if not (early(j) and k < 2):
                    pe.wait_ge(silu_ready, n - 1)
                three(h_bank[k % 2][:], we_hi[i][:, 0:P], we_lo[i][:, 0:P], mT_hi[:, cols], mT_lo[:, cols],
                      True, True).then_inc(h_full, 1)
                if not (early(j) and k < 2):
                    pe.wait_ge(s_u_ready, n - 1)
                three(u_bank[k % 2][:], we_hi[i][:, P:2 * P], we_lo[i][:, P:2 * P], mT_hi[:, cols], mT_lo[:, cols],
                      True, True).then_inc(u_full, 1)

            def down(j, k, stop=False):
                n = j * STEPS + k
                if isinstance(j, int) and n < FEW:
                    i, c = FIRST[n]
                    pe.wait_ge(dn_lo_ready, i + 1)
                else:
                    i, c = LATER[k]
                    if c == 0:
                        pe.wait_ge(dn_lo_ready, j * 2 + (i + 1) - (2 if k < 0 else 0))
                pe.wait_ge(act_lo_ready, n + 1)
                start = isinstance(j, int) and n < FEW and i == 0
                three(acc[c][:], we_hi[i][:, 2 * P:], we_lo[i][:, 2 * P:], act_hi[k % 4], act_lo[k % 4],
                      start, stop).then_inc(down_full, 1)

            up(0, 0)
            attend(CH - 1, TPC - 1)
            turn_combine(0)
            pe.wait_ge(y_ready, NT)
            up(0, 1)
            up(0, 2)
            turn_x1(CH - 1)
            up(0, 3)
            ffn_up(CH - 1, 0)
            ffn_up(CH - 1, 1)
            up(0, 4)
            ffn_down(CH - 1)
            down(0, 0)
            up(0, 5)
            down(0, 1)
            turn_xm(CH - 2)
            up(0, 6)
            down(0, 2)
            route(CH - 2)
            up(0, 7)
            down(0, 3)
            up(0, 8)
            turn_xm(CH - 1)
            down(0, 4)
            route(CH - 1)
            for k in range(9, 12):
                up(0, k)
                down(0, k - LAG)
            up(0, 12)
            pe.wait_ge(logits_ready, CH - 1)
            down(0, 8)
            up(0, 13)
            down(0, 9)
            turn_combine(1)
            pe.wait_ge(comb_T_ready, 2)
            first_weights(CH // 2)
            up(0, 14)
            pe.wait_ge(first_ready, 1)
            first_weights(CH // 2 + 1)
            up(0, 15)
            pe.wait_ge(first_ready, 2)
            down(0, 10)
            down(0, 11)

            for k in range(STEPS):
                up(2, k)
                down(2, k - LAG)
            with pe.Fori(3, NX // 2) as j:
                for k in range(STEPS):
                    up(j, k)
                    down(j, k - LAG)
            for k in range(-LAG, 0):
                down(NX // 2, k, stop=True)
            for c in range(CH):
                pe.wait_ge(acc_copied[c], 1)
                pe.wait_ge(s_u_ready, NX * CH)
                dst = (h_bank + u_bank)[c]
                src = q_flat[:, c * CW:(c + 1) * CW]
                for t in range(TPC):
                    last = pe.transpose(dst[:, t * P:(t + 1) * P], src[:, t * P:(t + 1) * P], ident[:])
                last.then_inc(out_turned, 1)


_INS = ['x', 'ctx_1024', 'mask_BxS2_ff1', 'L0_xattn_Wq', 'L0_xattn_Wk', 'L0_xattn_Wv', 'L0_xattn_Wo', 'L0_xattn_W1',
        'L0_xattn_b1', 'L0_xattn_W2', 'L0_xattn_b2', 'L0_xattn_gamma', 'L0_xattn_beta', 'L0_ffn_router_w',
        'L0_ffn_bias', 'L0_ffn_gate_w', 'L0_ffn_up_w', 'L0_ffn_down_w', 'L0_ffn_sh_gate_w', 'L0_ffn_sh_up_w',
        'L0_ffn_sh_down_w']


def kernel(**inputs):
    import concourse.bacc as bacc
    from concourse.bass_utils import run_bass_kernel_spmd

    nc = bacc.Bacc("TRN2", target_bir_lowering=False, num_devices=1)
    arrays, args = {}, []
    for name in _INS:
        a = np.ascontiguousarray(inputs[name])
        arrays[f"in_{name}"] = a
        args.append(nc.dram_tensor(f"in_{name}", a.shape, mybir.dt.from_np(a.dtype), kind="ExternalInput").ap())
    args.append(nc.dram_tensor("out_x", (NB, SEQ, P), F32, kind="ExternalOutput").ap())
    build(nc, *args)
    r = run_bass_kernel_spmd(nc, [arrays], core_ids=[0])
    return r.results[0]["out_x"]
```
